# Optimizing a Trainium2 kernel written in Bass

```python
import numpy as np
import jax
import jax.numpy as jnp

def _softmax(x, axis=-1):
    return jax.nn.softmax(x, axis=axis)
def _gelu(x):
    return jax.nn.gelu(x, approximate=True)
def _silu(x):
    return jax.nn.silu(x)
def _sigmoid(x):
    return jax.nn.sigmoid(x)
def _layernorm(x, axis=-1, eps=1e-5):
    m = jnp.mean(x, axis=axis, keepdims=True)
    v = jnp.var(x, axis=axis, keepdims=True)
    return (x - m) / jnp.sqrt(v + eps)
def _scatter_add(tgt, idx, src, axis=0):
    return tgt.at[idx].add(src)
def _segment_sum(src, seg, n):
    return jax.ops.segment_sum(src, seg, n)

kernel_name = 'mk_conv_preact_d2_conv_nhwc64_f3f681'

def setup_inputs(seed: int = 0):
    np.random.seed(seed)
    _w = jnp.asarray
    def _rec_inputs():
        import jax
        import jax.numpy as jnp
        _gk = jax.random.key(seed)
        x = -0.000125 + 0.9999 * jax.random.normal(jax.random.fold_in(_gk, 1), (8, 256, 256, 64), jnp.float32)
        return x
    x = _rec_inputs()
    def _L0_conv_setup():
        import jax, jax.numpy as jnp
        import numpy as np
        N, R, C_IN, C_OUT, MODES = (8, 256, 64, 64, 16)
        key = jax.random.key(seed)
        k1, k2, k3, k4, k5 = jax.random.split(key, 5)
        std = 1.0 / (C_IN * C_OUT) * np.sqrt(2.0)
        return {'X': jax.random.normal(k1, (N, R, R, C_IN), dtype=jnp.float32), 'W_res': jax.random.normal(k2, (C_IN, C_OUT), dtype=jnp.float32) / np.sqrt(C_IN), 'b_res': jax.random.normal(k3, (C_OUT,), dtype=jnp.float32) * 0.01, 'fw0': jax.random.normal(k4, (C_IN, C_OUT, MODES, MODES, 2), dtype=jnp.float32) * std, 'fw1': jax.random.normal(k5, (C_IN, C_OUT, MODES, MODES, 2), dtype=jnp.float32) * std}
    _L0_conv_all = _L0_conv_setup()
    _L0_conv_in = {k: v for k, v in _L0_conv_all.items() if k in ('W_res', 'b_res', 'fw0', 'fw1', )}
    del _L0_conv_all

    def _L1_conv_setup():
        import jax, jax.numpy as jnp
        import numpy as np
        M0F, M0B, M1 = (16, 16, 17)
        key = jax.random.key(seed)
        k1, k2, k3 = jax.random.split(key, 3)
        X = jax.random.normal(k1, (16, 128, 128, 64), dtype=jnp.float32)
        kernel_re = jax.random.uniform(k2, (32, 17, 64, 64), dtype=jnp.float32)
        kernel_im = jax.random.uniform(k3, (32, 17, 64, 64), dtype=jnp.float32)
        return {'X': X, 'kernel_re': kernel_re, 'kernel_im': kernel_im}
    _L1_conv_all = _L1_conv_setup()
    _L1_conv_in = {k: v for k, v in _L1_conv_all.items() if k in ('kernel_re', 'kernel_im', )}
    del _L1_conv_all

    return {
        "x": x,
        "L0_conv_W_res": _L0_conv_in["W_res"],
        "L0_conv_b_res": _L0_conv_in["b_res"],
        "L0_conv_fw0": _L0_conv_in["fw0"],
        "L0_conv_fw1": _L0_conv_in["fw1"],
        "L1_conv_kernel_re": _L1_conv_in["kernel_re"],
        "L1_conv_kernel_im": _L1_conv_in["kernel_im"],
    }

def reference(x, L0_conv_W_res, L0_conv_b_res, L0_conv_fw0, L0_conv_fw1, L1_conv_kernel_re, L1_conv_kernel_im):
    import jax
    import jax.numpy as jnp
    def _L0_conv_ref(X, W_res, b_res, fw0, fw1):
        import jax, jax.numpy as jnp
        import numpy as np
        N, R, C_IN, C_OUT, MODES = (8, 256, 64, 64, 16)
        n, r, _, _ = X.shape
        modes = fw0.shape[2]
        out_dim = fw0.shape[1]
        res = X @ W_res + b_res
        Xc = jnp.transpose(X, (0, 3, 1, 2))
        X_ft = jnp.fft.rfft2(Xc, s=(r, r), norm='ortho')
        w0 = fw0[..., 0] + 1j * fw0[..., 1]
        w1 = fw1[..., 0] + 1j * fw1[..., 1]
        top = jnp.einsum('bixy,ioxy->boxy', X_ft[:, :, :modes, :modes], w0)
        bot = jnp.einsum('bixy,ioxy->boxy', X_ft[:, :, r - modes:, :modes], w1)
        out_ft = jnp.zeros((n, out_dim, r, r // 2 + 1), dtype=X_ft.dtype)
        out_ft = out_ft.at[:, :, :modes, :modes].set(top)
        out_ft = out_ft.at[:, :, r - modes:, :modes].set(bot)
        Xo = jnp.fft.irfft2(out_ft, s=(r, r), norm='ortho')
        Xo = jnp.transpose(Xo, (0, 2, 3, 1))
        return jax.nn.silu(Xo + res)

    def _L1_conv_ref(X, kernel_re, kernel_im):
        import jax, jax.numpy as jnp
        import numpy as np
        M0F, M0B, M1 = (16, 16, 17)
        kernel = kernel_re + 1j * kernel_im
        Co = kernel.shape[-2]
        s1, s2 = (X.shape[-3], X.shape[-2])
        Xf = jnp.fft.rfftn(X, axes=(-3, -2), norm='forward')
        Yf = jnp.zeros(Xf.shape[:-1] + (Co,), dtype=Xf.dtype)
        Yf = Yf.at[:, :M0F, :M1].set(jnp.einsum('xyij,bxyj->bxyi', kernel[:M0F, :M1], Xf[:, :M0F, :M1]))
        Yf = Yf.at[:, -M0B:, :M1].set(jnp.einsum('xyij,bxyj->bxyi', kernel[-M0B:, :M1], Xf[:, -M0B:, :M1]))
        return jnp.fft.irfftn(Yf, axes=(-3, -2), s=(s1, s2), norm='forward')

    def _gn(v, G=32, eps=1e-5):
        B_, H_, W_, C_ = v.shape
        g = v.reshape(B_, H_, W_, G, C_ // G)
        m = jnp.mean(g, axis=(1, 2, 4), keepdims=True)
        s = jnp.var(g, axis=(1, 2, 4), keepdims=True)
        return ((g - m) / jnp.sqrt(s + eps)).reshape(v.shape)

    def _ln_c(v, eps=1e-6):
        m = jnp.mean(v, axis=-1, keepdims=True)
        s = jnp.var(v, axis=-1, keepdims=True)
        return (v - m) / jnp.sqrt(s + eps)

    def _ln_t(v, eps=1e-5):
        m = jnp.mean(v, axis=-1, keepdims=True)
        s = jnp.var(v, axis=-1, keepdims=True)
        return (v - m) / jnp.sqrt(s + eps)

    def _to_tokens(v):
        B_, H_, W_, C_ = v.shape
        return v.reshape(B_, H_ * W_, C_)
    def _from_tokens(t, like):
        return t.reshape(like.shape)

    x = x + _L0_conv_ref(_gn(x), L0_conv_W_res, L0_conv_b_res, L0_conv_fw0, L0_conv_fw1)
    x = x + _L1_conv_ref(_gn(x), L1_conv_kernel_re, L1_conv_kernel_im)
    return x


_drawn_inputs = setup_inputs


def setup_inputs(seed=0):
    import zlib

    import numpy as np

    out = dict(_drawn_inputs(seed))
    spreads = {}
    factors = {'L0_conv_b_res': 8.0, 'L0_conv_fw0': 64.0, 'L0_conv_fw1': 64.0}
    for name, (base, spread) in spreads.items():
        noise = np.random.default_rng([zlib.crc32(name.encode()), seed]).standard_normal(out[name].shape)
        drawn = base * np.exp(spread * noise) if base else spread * noise
        out[name] = jnp.asarray(drawn.astype(out[name].dtype))
    for name, factor in factors.items():
        out[name] = (out[name] * factor).astype(out[name].dtype)
    return out
```

```python
from contextlib import ExitStack

import numpy as np

import concourse.bass as bass
from concourse import mybir

F32 = mybir.dt.float32
F32R = mybir.dt.float32r
ALU = mybir.AluOpType
ACT = mybir.ActivationFunctionType
AX = mybir.AxisListType

P = 128
B, H, W, C = 8, 256, 256, 64
J = W // P
JC = J * C
HALF = H // P
KX = 32
RI = 2
PIX = H * W
EPS = 1e-5

ROWS = 16
CHUNKS = H // ROWS
UNIT = CHUNKS // HALF
NCH = B * CHUNKS
BROWS = 4
BANKS = ROWS // BROWS
NB = BROWS * JC
SLOTS = 4
GC = 8


class Layer:

    def __init__(self, ky, groups):
        self.KY = ky
        self.KYR = 2 * ky
        self.NG = groups
        self.GP = P // groups
        self.LO = self.GP
        self.K = self.LO + self.KYR
        self.M = KX * ky
        self.NQ = self.M // 2 // 8
        self.RM = 4
        self.R = self.M // (2 * 4 * self.RM)
        self.RR = C // (groups * GC)
        self.pieces = [(a, min(a + 8, ky)) for a in range(0, ky, 8)] if ky % 8 == 0 else [(0, 6), (6, 12), (12, 17)]


L0 = Layer(16, 4)
L1 = Layer(17, 2)


def tables():
    out = {"ident": np.eye(P)}
    kx = np.concatenate([np.arange(16), np.arange(-16, 0)])
    h = np.arange(H)
    ph = 2 * np.pi * ((kx[None, :] * h[:, None]) % H) / H
    c, s = np.cos(ph), np.sin(ph)
    fh = np.stack([np.concatenate([c, -s], 1), np.concatenate([-s, -c], 1)], 1)
    out["fwd_h"] = fh.reshape(HALF, P, 2, 2 * KX).transpose(1, 0, 2, 3).reshape(P, -1)
    out["inv_h"] = np.concatenate([c, -s], 1).T
    w = (J * np.arange(P)[None, :] + np.arange(J)[:, None])
    for n, lay in enumerate((L0, L1)):
        ky = np.arange(lay.KY)
        pw = 2 * np.pi * ((ky[None, None] * w[..., None]) % W) / W
        f = np.concatenate([np.cos(pw), np.sin(pw)], -1)
        out[f"fwd_w{n}"] = f.transpose(1, 0, 2).reshape(P, -1)
        m = np.tile(np.where(ky == 0, 1.0, 2.0), 2) / PIX
        g = (f * m).transpose(2, 0, 1)
        k = np.zeros((lay.K, J, P))
        k[:lay.KYR] = g
        k[lay.LO:] = g
        out[f"inv_w{n}"] = k.reshape(lay.K, -1)
    pair = np.arange(P) // 2
    out["pairs"] = (pair[:C, None] == (np.arange(P) % C // 2)[None, :]).astype(float)
    out["ones"] = np.ones((P, 8))
    return {k: np.ascontiguousarray(v, np.float32) for k, v in out.items()}


class Tiles:

    def __init__(self, nc, tag):
        self.nc, self.tag, self.stack = nc, tag, ExitStack()

    def __enter__(self):
        return self

    def __exit__(self, *a):
        return self.stack.__exit__(*a)

    def sb(self, name, shape, dt=F32):
        return self.stack.enter_context(self.nc.sbuf_tensor(f"{self.tag}_{name}", shape, dt))

    def ps(self, name, shape):
        return self.stack.enter_context(self.nc.psum_tensor(f"{self.tag}_{name}", shape, F32))

    def sem(self, name):
        return self.stack.enter_context(self.nc.semaphore(f"{self.tag}_{name}"))

    def sems(self, name, n):
        return [self.sem(f"{name}{i}") for i in range(n)]


def settle(eng, sem):
    eng.sem_inc(sem, 1)


def load_rows(eng, dst, src, sem):
    for h in range(0, ROWS, ROWS // 2):
        eng.dma_start(dst[:, h:h + ROWS // 2], src[:, h:h + ROWS // 2]).then_inc(sem, 16)


LOADED = 32


def load_constants(nc, d, k):
    with Tiles(nc, "c") as t:
        loaded, hi_done, split = t.sem("loaded"), t.sem("hi_done"), t.sem("split")
        raw = {n: t.sb(f"raw{n}", [lay.K, J * P]) for n, lay in ((0, L0), (1, L1))}
        pairs = [(k["ident"], d["ident"]), (k["fwd_h"], d["fwd_h"]), (k["inv_h"], d["inv_h"]),
                 (k["fwd_w0"], d["fwd_w0"]), (k["fwd_w1"], d["fwd_w1"]), (k["pairs"], d["pairs"]),
                 (k["ones"], d["ones"]), (raw[0], d["inv_w0"]), (raw[1], d["inv_w1"])]
        with nc.Block() as block:
            @block.sync
            def _(sp):
                for dst, src in pairs:
                    sp.dma_start(dst[:], src).then_inc(loaded, 16)
                sp.wait_ge(hi_done, 1)
                for j in range(J):
                    sp.dma_start(k["wdiag"][j * C:(j + 1) * C, j * C:(j + 1) * C], d["W_res"]).then_inc(loaded, 16)
                sp.dma_start(k["wres"][:], d["W_res"]).then_inc(loaded, 16)
                sp.dma_start(k["bias"][:], d["b_res"].rearrange("(a c) -> a c", a=1).broadcast_to([B, C])).then_inc(loaded, 16)
                sp.wait_ge(loaded, 16 * (len(pairs) + J + 2))

            @block.vector
            def _(dve):
                nc.vector.memset(k["wdiag"][:], 0.0).then_inc(hi_done, 1)
                dve.wait_ge(loaded, 16 * (len(pairs) + J + 2))
                for n in range(2):
                    nc.vector.tensor_copy(k[f"inv_w{n}h"][:], raw[n][:]).then_inc(hi_done, 1)
                dve.wait_ge(hi_done, 3)
                for n in range(2):
                    nc.vector.tensor_tensor(k[f"inv_w{n}l"][:], raw[n][:], k[f"inv_w{n}h"][:].bitcast(F32),
                                            ALU.subtract).then_inc(split, 1)


def forward_w0(nc, lay, k, x_dram, t_dram, sq, fw_dram, fw_loaded):
    with Tiles(nc, "a") as t:
        x = t.sb("x", [P, SLOTS, ROWS, JC])
        q = t.sb("q", [P, 2, ROWS, JC])
        part = t.sb("part", [P, UNIT, C])
        ts = t.sb("ts", [P, 2, 512])
        tp = t.ps("tp", [P, 2, 512])
        loaded, stored = t.sems("loaded", SLOTS), t.sems("stored", 2)
        names = ("summed", "copied", "squared", "reduced", "final", "tick")
        summed, copied, squared, reduced, final, tick = (t.sem(n) for n in names)
        PAIRS = SLOTS // 2
        N = NCH // SLOTS
        with nc.Block() as block:
            @block.sync
            def _(sp):
                with sp.Fori(0, N) as i:
                    for s in range(SLOTS):
                        if s % 2 == 0:
                            sp.wait_ge(summed, PAIRS * i + s // 2 + 1)
                            settle(sp, tick)
                            sp.wait_ge(squared, SLOTS * i + s + 2)
                        load_rows(sp, x[:, s], x_dram[SLOTS * i + s], loaded[s])

            @block.gpsimd
            def _(pool):
                with pool.Fori(0, N) as i:
                    for r in range(PAIRS):
                        pool.wait_ge(copied, PAIRS * i + r + 1 + 2)
                        for g in range(4):
                            pool.dma_start(t_dram[4 * (PAIRS * i + r) + g], ts[32 * g:32 * g + lay.KYR, r].rearrange("p (h c) -> p h c", c=C)).then_inc(stored[r], 16)
                for r in range(PAIRS):
                    pool.wait_ge(stored[r], 64 * N)

            @block.tensor
            def _(pe):
                pe.sem_inc(summed, PAIRS)
                with pe.Fori(0, N) as i:
                    for r in range(PAIRS):
                        for s in (2 * r, 2 * r + 1):
                            pe.wait_ge(loaded[s], LOADED * (i + 1))
                        pe.wait_ge(copied, PAIRS * i + r + 1)
                        for j in range(J):
                            for g in range(4):
                                s, h = 2 * r + g // 2, 8 * (g % 2)
                                mm = nc.tensor.matmul(tp[32 * g:32 * g + lay.KYR, r], k["fwd_w0"][:, j * lay.KYR:(j + 1) * lay.KYR],
                                                      x[:, s, h:h + 8, j * C:(j + 1) * C], start=(j == 0), stop=(j == J - 1))
                        mm.then_inc(summed, 1)

            @block.scalar
            def _(act):
                act.sem_inc(copied, PAIRS)
                act.sem_inc(squared, SLOTS)
                for half in range(2):
                    for o in range(0, C, C // 4):
                        cols = slice(o * L0.M, (o + C // 4) * L0.M)
                        act.dma_start(k["fw"][half * C:(half + 1) * C, cols], fw_dram[half][:, cols]).then_inc(fw_loaded, 16)
                with act.Fori(0, N) as i:
                    for s in range(SLOTS):
                        act.wait_ge(loaded[s], LOADED * (i + 1))
                        act.wait_ge(reduced, SLOTS * i + s + 1)
                        nc.scalar.activation(q[:, s % 2], x[:, s], ACT.Square).then_inc(squared, 1)
                        if s % 2:
                            r = s // 2
                            act.wait_ge(summed, PAIRS * i + r + 1 + PAIRS)
                            act.wait_ge(stored[r], 64 * i)
                            nc.scalar.activation(ts[:, r], tp[:, r], ACT.Copy).then_inc(copied, 1)

            @block.vector
            def _(dve):
                dve.sem_inc(reduced, 2)
                with dve.Fori(0, B * HALF) as u:
                    for s in range(UNIT):
                        dve.wait_ge(squared, UNIT * u + s + 1 + SLOTS)
                        if s == 0:
                            dve.wait_ge(final, u)
                        nc.vector.tensor_reduce(part[:, s], q[:, s % 2].rearrange("p h (j c) -> p c h j", j=J),
                                                AX.XY, ALU.add).then_inc(reduced, 1)
                    dve.wait_ge(reduced, UNIT * (u + 1) + 2)
                    nc.vector.tensor_reduce(sq[:, u], part[:].rearrange("p n c -> p c n"), AX.X, ALU.add).then_inc(final, 1)


def forward_h(nc, lay, tag, k, t_dram, xh_dram):
    with Tiles(nc, tag) as t:
        u = t.sb("u", [P, 2, HALF, lay.KYR * C])
        xs = t.sb("xs", [2 * KX, 2, lay.KY * C])
        NP = len(lay.pieces)
        ps = t.ps("ps", [P, 2, NP, 512])
        loaded, stored = t.sems("loaded", 2), t.sems("stored", 2)
        summed, copied = t.sem("summed"), t.sem("copied")
        with nc.Block() as block:
            @block.sync
            def _(sp):
                with sp.Fori(0, B // 2) as i:
                    for s in range(2):
                        sp.wait_ge(summed, 2 * i + s + 1)
                        for half in range(HALF):
                            sp.dma_start(u[:, s, half], t_dram[HALF * (2 * i + s) + half]).then_inc(loaded[s], 16)

            @block.tensor
            def _(pe):
                pe.sem_inc(summed, 2)
                with pe.Fori(0, B // 2) as i:
                    for s in range(2):
                        pe.wait_ge(loaded[s], 16 * HALF * (i + 1))
                        pe.wait_ge(copied, 2 * i + s + 1)
                        for n, (a, e) in enumerate(lay.pieces):
                            for half in range(HALF):
                                for cs in range(2):
                                    tab = k["fwd_h"][:, (half * 2 + cs) * 2 * KX:(half * 2 + cs + 1) * 2 * KX]
                                    mm = nc.tensor.matmul(ps[0:2 * KX, s, n, 0:(e - a) * C], tab,
                                                          u[:, s, half, (cs * lay.KY + a) * C:(cs * lay.KY + e) * C],
                                                          start=(half == 0 and cs == 0), stop=(half == HALF - 1 and cs == 1))
                        mm.then_inc(summed, 1)

            @block.scalar
            def _(act):
                act.sem_inc(copied, 2)
                with act.Fori(0, B // 2) as i:
                    for s in range(2):
                        act.wait_ge(summed, 2 * i + s + 1 + 2)
                        act.wait_ge(stored[s], 16 * 4 * i)
                        for n, (a, e) in enumerate(lay.pieces):
                            last = nc.scalar.activation(xs[:, s, a * C:e * C], ps[0:2 * KX, s, n, 0:(e - a) * C], ACT.Copy)
                        last.then_inc(copied, 1)

            @block.gpsimd
            def _(pool):
                with pool.Fori(0, B // 2) as i:
                    for s in range(2):
                        pool.wait_ge(copied, 2 * i + s + 1 + 2)
                        for half in range(2):
                            for ri in range(RI):
                                row = ri * KX + half * KX // 2
                                pool.dma_start(xh_dram[half][ri][2 * i + s], xs[row:row + KX // 2, s]).then_inc(stored[s], 16)
                for s in range(2):
                    pool.wait_ge(stored[s], 16 * 4 * (B // 2))


def mix_modes(nc, lay, tag, k, sq, xh_dram, y_dram, weights):
    M, NQ, R, RM = lay.M, lay.NQ, lay.R, lay.RM
    Q2 = 2
    NT = NQ // Q2
    LOOP = (R - 1) // 2
    YS = 4
    with Tiles(nc, tag) as t:
        xl = t.sb("xl", [P, NQ, 2, C])
        xt = t.sb("xt", [P, M // 2, RI, B])
        xr = t.sb("xr", [P, 2, 4, RM, 3, B])
        ys = t.sb("ys", [P, YS, 2, RM * C])
        st = t.sb("st", [P, 10, B])
        bt = t.sb("bt", [B, C])
        pt = t.ps("pt", [P, 2, 512])
        py = t.ps("py", [P, 2, 512])
        names = ("xl", "statistic_mm", "statistic", "turned", "scaled", "dc", "staged", "mixed", "copied", "zeroed", "ready", "tick")
        S = {n: t.sem(n) for n in names}
        stored = t.sems("stored", YS)
        wt = weights(nc, lay, t, k, S)
        DC, SSQ, MEAN, EX2, MSQ, VAR, SD, SCALE, SHIFT, SHIFT_DC = range(10)
        with nc.Block() as block:
            @block.sync
            def _(sp):
                for half in range(2):
                    sp.dma_start(xl[:, :, half], xh_dram[half]).then_inc(S["xl"], 16)
                wt.sync(sp)

            @block.gpsimd
            def _(pool):
                def store(r, z, n):
                    pool.wait_ge(S["ready"], r + 1)
                    for half in range(2):
                        for g in range(4):
                            pool.dma_start(y_dram[half * 4 + g][r], ys[32 * g:32 * g + RI * B, z, half]).then_inc(stored[z], 16)

                with pool.Fori(0, R // YS) as i:
                    for z in range(YS):
                        store(YS * i + z, z, i)
                for r in range(R // YS * YS, R):
                    store(r, r % YS, r // YS)
                for z in range(YS):
                    pool.wait_ge(stored[z], 16 * 8 * len(range(z, R, YS)))

            @block.tensor
            def _(pe):
                pe.sem_inc(S["mixed"], 1)
                pe.wait_ge(S["xl"], 32)

                def turn(q):
                    return nc.tensor.transpose(pt[:, (q // Q2) % 2, (q % Q2) * P:(q % Q2 + 1) * P],
                                               xl[:, q].rearrange("p a c -> p (a c)"), k["ident"][:])

                def mix_round(r, z):
                    wt.tensor(pe, r, z)
                    pe.wait_ge(S["staged"], r + 1)
                    pe.wait_ge(S["copied"], r)
                    settle(pe, S["tick"])
                    for m in range(RM):
                        for part in range(2):
                            for g in range(4):
                                for half in range(2):
                                    rows = slice(half * C, half * C + C)
                                    out = py[32 * g:32 * g + RI * B, half, (z * RM + m) * C:(z * RM + m + 1) * C]
                                    lhs = xr[rows, z, g, m, 1 - part:3 - part]
                                    mm = nc.tensor.matmul(out, lhs, wt.rhs(half, g, m, part, z), start=(part == 0),
                                                          stop=(part == 1), skip_group_check=True)
                    mm.then_inc(S["mixed"], 1)

                pe.wait_ge(S["zeroed"], 1)
                for b in range(B):
                    for half in range(HALF):
                        nc.tensor.matmul(py[0:C, 0, b:b + 1], sq[:, HALF * b + half], k["ones"][:, 0:1], start=(half == 0),
                                         stop=(half == HALF - 1), skip_group_check=True)
                for q in range(Q2):
                    turn(q).then_inc(S["turned"], 1)
                pe.wait_ge(S["statistic"], 2)
                nc.tensor.matmul(py[:, 1, 0:2 * B], k["pairs"][:], st[0:C, DC:SSQ + 1], start=True, stop=True,
                                 skip_group_check=True).then_inc(S["statistic_mm"], 1)
                if lay is L0:
                    pe.wait_ge(S["statistic"], 9)
                    nc.tensor.matmul(py[0:B, 1, 128:128 + C], st[0:C, SHIFT], k["wres"][:], start=True, stop=True,
                                     skip_group_check=True).then_inc(S["statistic_mm"], 1)
                for n in range(1, NT):
                    if n >= 2:
                        pe.wait_ge(S["scaled"], n - 1)
                    for q in range(Q2 * n, Q2 * n + Q2):
                        turn(q).then_inc(S["turned"], 1)
                wt.tensor_start(pe)
                with pe.Fori(0, LOOP) as i:
                    for z in range(2):
                        wt.tensor_next(pe, 2 * i + z + 1, 1 - z, i + z)
                        mix_round(2 * i + z, z)
                for r in range(2 * LOOP, R):
                    if r + 1 < R:
                        wt.tensor_next(pe, r + 1, (r + 1) % 2, (r + 1) // 2)
                    mix_round(r, r % 2)

            @block.scalar
            def _(act):
                act.wait_ge(S["statistic"], 6)
                nc.scalar.activation(st[:, SD], st[:, VAR], ACT.Sqrt).then_inc(S["statistic"], 1)
                wt.scalar(act)

            @block.vector
            def _(dve):
                nc.vector.memset(py[:], 0.0).then_inc(S["zeroed"], 1)
                dve.wait_ge(S["turned"], Q2)
                first = pt[:, 0, 0:P].rearrange("p (r b m) -> p r b m", r=RI, b=B)
                nc.vector.tensor_copy(st[0:C, DC], first[0:C, 0, :, 0]).then_inc(S["statistic"], 1)
                nc.vector.tensor_copy(st[0:C, SSQ], py[0:C, 0, 0:B]).then_inc(S["statistic"], 1)
                dve.wait_ge(S["statistic_mm"], 1)
                n = 1.0 / (2 * PIX)
                nc.vector.tensor_scalar(st[:, MEAN], py[:, 1, 0:B], n, None, ALU.mult).then_inc(S["statistic"], 1)
                nc.vector.tensor_scalar(st[:, EX2], py[:, 1, B:2 * B], n, EPS, ALU.mult, ALU.add).then_inc(S["statistic"], 1)
                dve.wait_ge(S["statistic"], 4)
                nc.vector.tensor_tensor(st[:, MSQ], st[:, MEAN], st[:, MEAN], ALU.mult).then_inc(S["statistic"], 1)
                dve.wait_ge(S["statistic"], 5)
                nc.vector.tensor_tensor(st[:, VAR], st[:, EX2], st[:, MSQ], ALU.subtract).then_inc(S["statistic"], 1)
                dve.wait_ge(S["statistic"], 7)
                nc.vector.reciprocal(st[:, SCALE], st[:, SD]).then_inc(S["statistic"], 1)
                dve.wait_ge(S["statistic"], 8)
                nc.vector.tensor_tensor(st[:, SHIFT], st[:, SCALE], st[:, MEAN], ALU.mult).then_inc(S["statistic"], 1)
                dve.wait_ge(S["statistic"], 9)
                nc.vector.tensor_scalar(st[:, SHIFT_DC], st[:, SHIFT], float(PIX), None, ALU.mult).then_inc(S["statistic"], 1)

                scale = st[:, SCALE].rearrange("p (a b) -> p a b", a=1).broadcast_to([P, 8, B])
                by_q = xt[:].rearrange("p (m q) r b -> p q r m b", m=8)
                for n in range(NT):
                    dve.wait_ge(S["turned"], Q2 * (n + 1))
                    for q in range(Q2):
                        for ri in range(RI):
                            src = pt[:, n % 2, q * P:(q + 1) * P].rearrange("p (r b m) -> p r m b", r=RI, b=B)[:, ri]
                            last = nc.vector.tensor_tensor(by_q[:, Q2 * n + q, ri], src, scale, ALU.mult)
                    last.then_inc(S["scaled"], 1)
                dve.wait_ge(S["scaled"], NT)
                dve.wait_ge(S["statistic"], 10)
                nc.vector.tensor_tensor(xt[0:C, 0, 0], xt[0:C, 0, 0], st[0:C, SHIFT_DC], ALU.subtract).then_inc(S["dc"], 1)
                if lay is L0:
                    dve.wait_ge(S["statistic_mm"], 2)
                    nc.vector.tensor_tensor(bt[:], k["bias"][:], py[0:B, 1, 128:128 + C], ALU.subtract).then_inc(S["dc"], 1)
                    for b in range(B):
                        nc.vector.tensor_scalar(k["wscaled"][:, b], k["wdiag"][:], st[:, SCALE, b:b + 1], None,
                                                ALU.mult).then_inc(S["dc"], 1)
                    dve.wait_ge(S["dc"], B + 2)
                else:
                    dve.wait_ge(S["dc"], 1)
                by_round = xt[:].rearrange("p (g r m) s b -> p r g m (s b)", g=4, r=R)

                def stage(r, z):
                    for m in range(RM):
                        nc.vector.tensor_copy(xr[:, z, :, m, 1:3].rearrange("p g s b -> p g (s b)"), by_round[:, r, :, m])
                        last = nc.vector.tensor_scalar(xr[:, z, :, m, 0], by_round[:, r, :, m, B:2 * B], -1.0, None, ALU.mult)
                    last.then_inc(S["staged"], 1)

                def copy_out(r, z, y, n):
                    dve.wait_ge(S["mixed"], r + 2)
                    dve.wait_ge(stored[y], 16 * 8 * n)
                    cp = nc.vector.tensor_copy(ys[:, y], py[:, :, z * RM * C:(z + 1) * RM * C])
                    cp.then_inc(S["copied"], 1)
                    if lay is L0 and isinstance(r, int) and r == 0:
                        dve.wait_ge(S["copied"], 1)
                        cp = nc.vector.scalar_tensor_tensor(out=ys[0:B, 0, 0, 0:C], in0=bt[:], scalar=float(PIX),
                                                            in1=ys[0:B, 0, 0, 0:C], op0=ALU.mult, op1=ALU.add)
                        cp.then_inc(S["ready"], 1)
                    else:
                        dve.wait_ge(S["copied"], r + 1)
                        dve.sem_inc(S["ready"], 1)

                def round_(r, z, y, n):
                    if not (isinstance(r, int) and r + 1 >= R):
                        dve.wait_ge(S["mixed"], r + 1)
                        stage(r + 1, 1 - z)
                    copy_out(r, z, y, n)

                stage(0, 0)
                for r in range(YS):
                    round_(r, r % 2, r, 0)
                FULL = (R - 1) // YS
                with dve.Fori(1, FULL) as i:
                    for y in range(YS):
                        round_(YS * i + y, y % 2, y, i)
                for r in range(YS * FULL, R):
                    round_(r, r % 2, r % YS, r // YS)


def each_round(eng, lay, body):
    with eng.Fori(0, lay.R // 2) as i:
        for z in range(2):
            body(2 * i + z, z)
    if lay.R % 2:
        body(lay.R - 1, 0)


class weights0:

    def __init__(self, nc, lay, t, k, S):
        self.nc, self.lay, self.k, self.S = nc, lay, k, S
        self.w = t.sb("w", [P, 2, 4 * lay.RM, RI * C])
        self.packed = t.sem("w_packed")

    def sync(self, sp):
        pass

    def tensor_start(self, pe):
        pass

    def tensor_next(self, pe, r, z, n):
        pass

    def tensor(self, pe, r, z):
        pe.wait_ge(self.packed, r + 1)

    def scalar(self, act):
        lay = self.lay
        act.wait_ge(self.k["fw_loaded"], 16 * 8)
        by_round = self.k["fw"][:].rearrange("p (o g r x) -> p r g x o", o=C, g=4, r=lay.R)

        def body(r, z):
            act.wait_ge(self.S["mixed"], r)
            dst = self.w[:, z].rearrange("p (g m) (i o) -> p g (m i) o", g=4, i=RI)
            self.nc.scalar.activation(dst, by_round[:, r], ACT.Copy).then_inc(self.packed, 1)
        each_round(act, lay, body)

    def rhs(self, half, g, m, part, z):
        return self.w[half * C:half * C + C, z, g * self.lay.RM + m, part * C:part * C + C]


class weights1:

    def __init__(self, nc, lay, t, k, S):
        self.nc, self.lay, self.k, self.S = nc, lay, k, S
        self.raw = t.sb("raw", [P, 2, 4 * lay.RM, 2, C])
        self.w = t.sb("w", [P, 2, 4 * lay.RM, P])
        self.ps = t.ps("pw", [P, 4, 512])
        self.loaded = t.sems("w_loaded", 2)
        self.turned, self.copied = t.sem("w_turned"), t.sem("w_copied")

    def sync(self, sp):
        def body(r, z):
            sp.wait_ge(self.turned, 4 * r)
            for ri in range(RI):
                for half in range(2):
                    for g in range(4):
                        sp.dma_start(self.raw[ri * C:(ri + 1) * C, z, 4 * g:4 * g + 4, half],
                                     self.k["kernel"][ri][half * 4 + g][r]).then_inc(self.loaded[z], 16)
        each_round(sp, self.lay, body)

    def tensor_start(self, pe):
        pe.sem_inc(self.turned, 4)
        self.tensor_next(pe, 0, 0, 0)

    def tensor_next(self, pe, r, z, n):
        pe.wait_ge(self.loaded[z], 256 * (n + 1))
        for b in range(4):
            pe.wait_ge(self.copied, 4 * r + b + 1)
            for q in range(4 * b, 4 * b + 4):
                mm = self.nc.tensor.transpose(self.ps[:, b, (q % 4) * P:(q % 4 + 1) * P], self.raw[:, z, q].rearrange("p a c -> p (a c)"), self.k["ident"][:])
            mm.then_inc(self.turned, 1)

    def tensor(self, pe, r, z):
        pe.wait_ge(self.copied, 4 * r + 8)

    def scalar(self, act):
        act.sem_inc(self.copied, 4)

        def body(r, z):
            act.wait_ge(self.S["mixed"], r)
            for b in range(4):
                act.wait_ge(self.turned, 4 * r + b + 5)
                self.nc.scalar.activation(self.w[:, z, 4 * b:4 * b + 4].rearrange("p q c -> p (q c)"), self.ps[:, b],
                                          ACT.Copy).then_inc(self.copied, 1)
        each_round(act, self.lay, body)

    def rhs(self, half, g, m, part, z):
        return self.w[half * C:half * C + C, z, g * self.lay.RM + m, part * C:part * C + C]


class InverseH:

    def __init__(self, nc, lay, t, k, y_dram):
        self.nc, self.lay, self.k, self.y_dram = nc, lay, k, y_dram
        self.gap = lay.LO > lay.KYR
        self.y = t.sb("y", [RI * KX, 2, lay.KY, C])
        self.g = t.sb("g", [P, 2, P, C], F32R)
        self.tab = t.sb("tab", [RI * KX, P])
        self.ps = t.ps("pg", [P, 2, 512])
        self.loaded, self.ready = t.sem("y_loaded"), t.sem("y_ready")
        self.summed, self.hi, self.lo, self.zeroed = (t.sem("g_" + n) for n in ("summed", "hi", "lo", "zeroed"))
        self.tick, self.tick_sp = t.sem("g_tick"), t.sem("g_tick_sp")

    def load(self, sp, b, v):
        sp.wait_ge(self.summed, self.lay.RR * v)
        settle(sp, self.tick_sp)
        sp.wait_ge(self.ready, 2 * v)
        for cs in range(2):
            for ri in range(RI):
                src = self.y_dram[ri if cs == 0 else 1 - ri][b]
                sp.dma_start(self.y[ri * KX:(ri + 1) * KX, cs].rearrange("p k c -> p (k c)"), src).then_inc(self.loaded, 16)

    def clear(self, dve):
        if self.gap:
            self.nc.vector.memset(self.g[:].bitcast(F32), 0.0).then_inc(self.zeroed, 1)

    def prepare(self, dve, v, half):
        dve.wait_ge(self.summed, self.lay.RR * v)
        self.nc.vector.tensor_copy(self.tab[:], self.k["inv_h"][:, half * P:(half + 1) * P] if isinstance(half, int)
                                   else self.k["inv_h"][:].rearrange("p (a h) -> p a h", a=HALF)[:, half]).then_inc(self.ready, 1)
        dve.wait_ge(self.loaded, 64 * (v + 1))
        self.nc.vector.tensor_scalar(self.y[0:KX, 1], self.y[0:KX, 1], -1.0, None, ALU.mult).then_inc(self.ready, 1)

    def tensor(self, pe, r, v):
        lay = self.lay
        pe.wait_ge(self.ready, 2 * v + 2)
        pe.wait_ge(self.lo, lay.RR * v + r)
        settle(pe, self.tick)
        for cc in range(GC):
            for g in range(lay.NG):
                c = (g * lay.RR + r) * GC + cc
                mm = self.nc.tensor.matmul(self.ps[lay.GP * g:lay.GP * g + lay.KYR, cc // 4, (cc % 4) * P:(cc % 4 + 1) * P],
                                           self.y[:, :, :, c].rearrange("p s k -> p (s k)"), self.tab[:],
                                           start=True, stop=True, skip_group_check=True)
        mm.then_inc(self.summed, 1)

    def cut(self, g, r):
        lay = self.lay
        c = (g * lay.RR + r) * GC
        return (self.ps[lay.GP * g:lay.GP * g + lay.KYR].rearrange("p k (c h) -> p h (k c)", h=P), slice(c, c + GC))

    def scalar(self, act, r, v, slot):
        lay = self.lay
        if self.gap:
            act.wait_ge(self.zeroed, 1)
        act.wait_ge(self.summed, lay.RR * v + r + 1)
        for g in range(lay.NG):
            src, cols = self.cut(g, r)
            last = self.nc.scalar.activation(self.g[0:lay.KYR, slot, :, cols], src, ACT.Copy)
        last.then_inc(self.hi, 1)

    def vector(self, dve, r, v, slot):
        lay = self.lay
        dve.wait_ge(self.hi, lay.RR * v + r + 1)
        for g in range(lay.NG):
            src, cols = self.cut(g, r)
            last = self.nc.vector.tensor_tensor(self.g[lay.LO:lay.LO + lay.KYR, slot, :, cols], src,
                                                self.g[0:lay.KYR, slot, :, cols].bitcast(F32), ALU.subtract)
        last.then_inc(self.lo, 1)

    def inverse_w(self, tables, z, slot, row):
        lay = self.lay
        out = z.rearrange("p (h j c) -> p j h c", j=J, c=C)
        for n, tab in enumerate(tables):
            for j in range(J):
                mm = self.nc.tensor.matmul(out[:, j], tab[:, j * P:(j + 1) * P], self.g[0:lay.K, slot, row:row + BROWS],
                                           start=(n == 0 and j == 0), stop=(n == 1), skip_group_check=True)
        return mm


def pixels0(nc, lay, k, x_dram, y_dram, x1_dram, t_dram, sq):
    with Tiles(nc, "b") as t:
        x = t.sb("x", [P, SLOTS, ROWS, JC])
        x1 = t.sb("x1", [P, SLOTS, ROWS, JC])
        xt = t.sb("xt", [P, 2, NB])
        q = t.sb("q", [P, 2, ROWS, JC])
        part = t.sb("part", [P, UNIT, C])
        ts = t.sb("ts", [P, 2, 512])
        pt = t.ps("pt", [P, 2, NB])
        z = t.ps("z", [P, 2, NB])
        tp = t.ps("tp", [P, 2, 512])
        G = InverseH(nc, lay, t, k, y_dram)
        loaded, x1_stored, t_stored = t.sems("loaded", SLOTS), t.sems("x1_stored", SLOTS), t.sems("t_stored", 2)
        names = ("turned", "turned_copied", "pixels", "silu", "added", "summed", "t_copied", "squared", "reduced", "final")
        turned, turned_copied, pixels, silu, added, summed, t_copied, squared, reduced, final = (t.sem(n) for n in names)
        tabs = (k["inv_w0h"], k["inv_w0l"])
        NU = B * HALF
        ROUND_AT = {2: 0, 5: 1}
        assert lay.RR == 2

        def units(eng, body):
            with eng.Fori(0, NU - 1) as u:
                body(u, False)
            body(NU - 1, True)

        with nc.Block() as block:
            @block.sync
            def _(sp):
                def x1_store(n, s):
                    sp.wait_ge(added, n + 1)
                    sp.dma_start(x1_dram[n], x1[:, s % SLOTS].rearrange("p h c -> p (h c)")).then_inc(x1_stored[s % SLOTS], 16)

                def t_store(n, s):
                    sp.wait_ge(t_copied, n + 1 + 2)
                    for g in range(2):
                        sp.dma_start(t_dram[2 * n + g], ts[C * g:C * g + L1.KYR, s % 2].rearrange("p (h c) -> p h c", c=C)).then_inc(t_stored[s % 2], 16)

                def unit(u, first, last):
                    if not last:
                        G.load(sp, (u + 1) // HALF, u + 1)
                    for s in range(UNIT):
                        n = UNIT * u + s
                        if not (first and s == 0):
                            sp.wait_ge(added, n)
                        if not (last and s + 3 >= UNIT):
                            load_rows(sp, x[:, (s + 3) % SLOTS], x_dram[n + 3], loaded[(s + 3) % SLOTS])
                        if not (first and s < 1):
                            x1_store(n - 1, s + SLOTS - 1)
                        if not (first and s < 2):
                            t_store(n - 2, s)

                G.load(sp, 0, 0)
                for s in range(SLOTS - 1):
                    load_rows(sp, x[:, s], x_dram[s], loaded[s])
                unit(0, True, False)
                with sp.Fori(1, NU - 1) as u:
                    unit(u, False, False)
                unit(NU - 1, False, True)
                x1_store(NCH - 1, SLOTS - 1)
                t_store(NCH - 2, 0)
                t_store(NCH - 1, 1)
                for s in range(SLOTS):
                    sp.wait_ge(x1_stored[s], 16 * (NCH // SLOTS))
                for s in range(2):
                    sp.wait_ge(t_stored[s], 32 * (NCH // 2))

            @block.tensor
            def _(pe):
                pe.sem_inc(summed, SLOTS)
                for r in range(lay.RR):
                    G.tensor(pe, r, 0)

                def turn(u, s, m):
                    if m == 0:
                        pe.wait_ge(loaded[s % SLOTS], LOADED * (2 * u + s // SLOTS + 1))
                    for h in range(BROWS):
                        tr = nc.tensor.transpose(pt[:, m % 2, h * P:(h + 1) * P], x[:, s % SLOTS, BROWS * m + h], k["ident"][:])
                    tr.then_inc(turned, 1)

                def forward(u, s):
                    n = UNIT * u + s
                    pe.wait_ge(added, n + 1)
                    pe.wait_ge(t_copied, n + 1)
                    for j in range(J):
                        for g in range(2):
                            mm = nc.tensor.matmul(tp[C * g:C * g + L1.KYR, s % 2], k["fwd_w1"][:, j * L1.KYR:(j + 1) * L1.KYR],
                                                  x1[:, s % SLOTS, 8 * g:8 * g + 8, j * C:(j + 1) * C], start=(j == 0), stop=(j == J - 1))
                    mm.then_inc(summed, 1)

                def body(u, last):
                    turn(u, 0, 0)
                    pe.wait_ge(G.lo, lay.RR * (u + 1))
                    for s in range(UNIT):
                        for m in range(BANKS):
                            bank = BANKS * (UNIT * u + s) + m
                            nxt = BANKS * s + m + 1
                            if nxt < UNIT * BANKS:
                                turn(u, nxt // BANKS, nxt % BANKS)
                            pe.wait_ge(silu, bank + 1)
                            G.inverse_w(tabs, z[:, m % 2], u % 2, ROWS * s + BROWS * m)
                            pe.wait_ge(turned_copied, bank + 1)
                            for h in range(BROWS):
                                cols = slice(h * P, (h + 1) * P)
                                mm = nc.tensor.matmul(z[:, m % 2, cols], xt[:, m % 2, cols], k["wscaled"][:, u // HALF],
                                                      start=False, stop=True, skip_group_check=True)
                            mm.then_inc(pixels, 1)
                            if m == 1 and s:
                                forward(u, s - 1)
                        if s in ROUND_AT and not last:
                            G.tensor(pe, ROUND_AT[s], u + 1)
                    forward(u, UNIT - 1)

                units(pe, body)

            @block.scalar
            def _(act):
                act.sem_inc(silu, 2)
                act.sem_inc(t_copied, 2)
                act.sem_inc(squared, SLOTS)
                for r in range(lay.RR):
                    G.scalar(act, r, 0, 0)

                def after(u, s):
                    n = UNIT * u + s
                    act.wait_ge(added, n + 1)
                    act.wait_ge(reduced, n + 1)
                    nc.scalar.activation(q[:, s % 2], x1[:, s % SLOTS], ACT.Square).then_inc(squared, 1)
                    act.wait_ge(summed, n + 1 + SLOTS)
                    act.wait_ge(t_stored[s % 2], 32 * (UNIT // 2) * u + 32 * (s // 2))
                    for g in range(2):
                        rows = slice(C * g, C * g + L1.KYR)
                        last = nc.scalar.activation(ts[rows, s % 2], tp[rows, s % 2], ACT.Copy)
                    last.then_inc(t_copied, 1)

                def body(u, last):
                    for s in range(UNIT):
                        for m in range(BANKS):
                            n = UNIT * u + s
                            act.wait_ge(pixels, BANKS * n + m + 1)
                            if m == 0:
                                act.wait_ge(summed, n + 1)
                                act.wait_ge(squared, n + 1)
                                act.wait_ge(x1_stored[s % SLOTS], 32 * u + 16 * (s // SLOTS))
                            nc.scalar.activation(x1[:, s % SLOTS, BROWS * m:BROWS * (m + 1)].rearrange("p h c -> p (h c)"),
                                                 z[:, m % 2], ACT.Silu).then_inc(silu, 1)
                        if s:
                            after(u, s - 1)
                        if s in ROUND_AT and not last:
                            G.scalar(act, ROUND_AT[s], u + 1, (u + 1) % 2)
                    after(u, UNIT - 1)

                units(act, body)

            @block.gpsimd
            def _(pool):
                def body(u, last):
                    for s in range(UNIT):
                        pool.wait_ge(silu, BANKS * (UNIT * u + s + 1) + 2)
                        nc.gpsimd.tensor_tensor(x1[:, s % SLOTS], x1[:, s % SLOTS], x[:, s % SLOTS], ALU.add).then_inc(added, 1)

                with pool.Fori(0, NU) as u:
                    body(u, False)

            @block.vector
            def _(dve):
                dve.sem_inc(reduced, 2)
                G.clear(dve)
                G.prepare(dve, 0, 0)
                for r in range(lay.RR):
                    G.vector(dve, r, 0, 0)

                def reduce(u, s):
                    if s == 0:
                        dve.wait_ge(final, u)
                    dve.wait_ge(squared, UNIT * u + s + 1 + SLOTS)
                    nc.vector.tensor_reduce(part[:, s], q[:, s % 2].rearrange("p h (j c) -> p c h j", j=J),
                                            AX.XY, ALU.add).then_inc(reduced, 1)

                def body(u, last):
                    for s in range(UNIT):
                        for m in range(BANKS):
                            bank = BANKS * (UNIT * u + s) + m
                            dve.wait_ge(turned, bank + 1)
                            nc.vector.tensor_copy(xt[:, m % 2], pt[:, m % 2]).then_inc(turned_copied, 1)
                            if m == 1 and s >= 2:
                                reduce(u, s - 2)
                        if s in ROUND_AT and not last:
                            G.vector(dve, ROUND_AT[s], u + 1, (u + 1) % 2)
                        if s == 0 and not last:
                            G.prepare(dve, u + 1, (u + 1) % HALF)
                    reduce(u, UNIT - 2)
                    reduce(u, UNIT - 1)
                    dve.wait_ge(reduced, UNIT * (u + 1) + 2)
                    nc.vector.tensor_reduce(sq[:, u], part[:].rearrange("p n c -> p c n"), AX.X, ALU.add).then_inc(final, 1)

                units(dve, body)


def pixels1(nc, lay, k, x1_dram, y_dram, out_dram):
    DEEP = UNIT
    with Tiles(nc, "p") as t:
        x = t.sb("x", [P, DEEP, ROWS, JC])
        z = t.ps("z", [P, 4, NB])
        G = InverseH(nc, lay, t, k, y_dram)
        loaded, stored = t.sems("loaded", DEEP), t.sems("stored", DEEP)
        spectral, added = t.sem("spectral"), t.sem("added")
        tabs = (k["inv_w1h"], k["inv_w1l"])
        NU = B * HALF
        ROUND_AT = {1: 0, 3: 1, 5: 2, 6: 3}
        assert lay.RR == 4

        def units(eng, body):
            with eng.Fori(0, NU - 1) as u:
                body(u, False)
            body(NU - 1, True)

        with nc.Block() as block:
            @block.sync
            def _(sp):
                def body(u, last):
                    for s in range(DEEP):
                        sp.wait_ge(stored[s], 16 * u)
                        sp.dma_start(x[:, s].rearrange("p h c -> p (h c)"), x1_dram[UNIT * u + s]).then_inc(loaded[s], 16)
                        if s == 0 and not last:
                            G.load(sp, (u + 1) // HALF, u + 1)

                G.load(sp, 0, 0)
                units(sp, body)

            @block.tensor
            def _(pe):
                for r in range(lay.RR):
                    G.tensor(pe, r, 0)

                def body(u, last):
                    pe.wait_ge(G.lo, lay.RR * (u + 1))
                    for s in range(UNIT):
                        for m in range(BANKS):
                            bank = BANKS * (UNIT * u + s) + m
                            pe.wait_ge(added, bank + 1)
                            G.inverse_w(tabs, z[:, m], u % 2, ROWS * s + BROWS * m).then_inc(spectral, 1)
                        if s in ROUND_AT and not last:
                            G.tensor(pe, ROUND_AT[s], u + 1)

                units(pe, body)

            @block.vector
            def _(dve):
                dve.sem_inc(added, 4)
                G.clear(dve)
                G.prepare(dve, 0, 0)
                for r in range(lay.RR):
                    G.vector(dve, r, 0, 0)

                def body(u, last):
                    for s in range(UNIT):
                        dve.wait_ge(loaded[s], 16 * u + 16)
                        for m in range(BANKS):
                            bank = BANKS * (UNIT * u + s) + m
                            dve.wait_ge(spectral, bank + 1)
                            rows = x[:, s, BROWS * m:BROWS * (m + 1)].rearrange("p h c -> p (h c)")
                            nc.vector.tensor_tensor(rows, rows, z[:, m], ALU.add).then_inc(added, 1)
                        if s == 0 and not last:
                            G.prepare(dve, u + 1, (u + 1) % HALF)
                        if s in ROUND_AT and not last:
                            G.vector(dve, ROUND_AT[s], u + 1, (u + 1) % 2)

                units(dve, body)

            @block.scalar
            def _(act):
                for r in range(lay.RR):
                    G.scalar(act, r, 0, 0)

                def body(u, last):
                    for s in range(UNIT):
                        act.wait_ge(added, BANKS * (UNIT * u + s + 1) + 4)
                        act.dma_start(out_dram[UNIT * u + s], x[:, s]).then_inc(stored[s], 16)
                        if s in ROUND_AT and not last:
                            G.scalar(act, ROUND_AT[s], u + 1, (u + 1) % 2)

                units(act, body)
                for s in range(DEEP):
                    act.wait_ge(stored[s], 16 * NU)


def build(nc, d, out):
    def scratch(name, shape):
        return nc.dram_tensor(name, shape, F32, kind="Internal").ap()

    t0 = scratch("t0", [B * H, L0.KYR, C])
    t1 = scratch("t1", [B * H, L1.KYR, C])
    x0h, y0 = scratch("x0h", [2, RI, B, L0.M // 2, C]), scratch("y0", [RI, B, L0.M, C])
    x1h, y1 = scratch("x1h", [2, RI, B, L1.M // 2, C]), scratch("y1", [RI, B, L1.M, C])
    x1 = scratch("x1", [NCH, P, ROWS * JC])
    image = lambda a: a.rearrange("b (k h) (p j) c -> (b k) p h (j c)", k=CHUNKS, j=J)
    by_image = lambda a: a.rearrange("r b (x y) c -> r b x (y c)", x=KX)
    by_half = lambda a: a.rearrange("a r b (x y) c -> a r b x (y c)", x=KX // 2)
    by_octet = lambda a: a.rearrange("a r b (m q) c -> a (r b m) q c", m=8)
    by_round = lambda a: a.rearrange("r b (g n m) c -> g n (r b) (m c)", g=8, m=4)
    t_rows = lambda a: a.rearrange("(n h) k c -> n k h c", h=8)
    t_halves = lambda a: a.rearrange("(n p) k c -> n p (k c)", p=P)

    with Tiles(nc, "k") as t:
        k = {"ident": t.sb("ident", [P, P]), "fwd_h": t.sb("fwd_h", [P, HALF * 2 * 2 * KX]),
             "inv_h": t.sb("inv_h", [RI * KX, H]), "pairs": t.sb("pairs", [C, P]), "ones": t.sb("ones", [P, 8]),
             "wdiag": t.sb("wdiag", [P, P]), "wres": t.sb("wres", [C, C]), "bias": t.sb("bias", [B, C]),
             "wscaled": t.sb("wscaled", [P, B, P])}
        for n, lay in enumerate((L0, L1)):
            k[f"fwd_w{n}"] = t.sb(f"fwd_w{n}", [P, J * lay.KYR])
            k[f"inv_w{n}h"] = t.sb(f"inv_w{n}h", [lay.K, J * P], F32R)
            k[f"inv_w{n}l"] = t.sb(f"inv_w{n}l", [lay.K, J * P], F32R)
        sq = t.sb("sq", [P, B * HALF, C])
        load_constants(nc, d, k)
        with Tiles(nc, "w") as tw:
            k["fw"] = tw.sb("fw", [P, C * L0.M])
            k["fw_loaded"] = tw.sem("fw_loaded")
            fw = [d[n].rearrange("i o x y r -> i (o x y r)") for n in ("fw0", "fw1")]
            forward_w0(nc, L0, k, image(d["x"]), t_rows(t0), sq, fw, k["fw_loaded"])
            forward_h(nc, L0, "h0", k, t_halves(t0), by_half(x0h))
            mix_modes(nc, L0, "m0", k, sq, by_octet(x0h), by_round(y0), weights0)
        pixels0(nc, L0, k, image(d["x"]), by_image(y0), x1, t_rows(t1), sq)
        k["kernel"] = [d[n].rearrange("x y o i -> (x y) o i").rearrange("(g n m) o i -> g n o m i", g=8, m=4)
                       for n in ("kernel_re", "kernel_im")]
        forward_h(nc, L1, "h1", k, t_halves(t1), by_half(x1h))
        mix_modes(nc, L1, "m1", k, sq, by_octet(x1h), by_round(y1), weights1)
        pixels1(nc, L1, k, x1, by_image(y1), image(out))


def kernel(x, L0_conv_W_res, L0_conv_b_res, L0_conv_fw0, L0_conv_fw1, L1_conv_kernel_re, L1_conv_kernel_im):
    import concourse.bacc as bacc
    from concourse.bass_utils import run_bass_kernel_spmd

    nc = bacc.Bacc("TRN2", target_bir_lowering=False, num_devices=1)
    arrays = {"x": x, "W_res": L0_conv_W_res, "b_res": L0_conv_b_res, "fw0": L0_conv_fw0, "fw1": L0_conv_fw1,
              "kernel_re": L1_conv_kernel_re, "kernel_im": L1_conv_kernel_im}
    arrays = {n: np.ascontiguousarray(a) for n, a in arrays.items()} | tables()
    maps, d = {}, {}
    for n, a in arrays.items():
        maps[f"in_{n}"] = a
        d[n] = nc.dram_tensor(f"in_{n}", a.shape, mybir.dt.from_np(a.dtype), kind="ExternalInput").ap()
    out = nc.dram_tensor("out", (B, H, W, C), F32, kind="ExternalOutput").ap()
    build(nc, d, out)
    r = run_bass_kernel_spmd(nc, [maps], core_ids=[0])
    return r.results[0]["out"]
```

```python
from contextlib import ExitStack

import numpy as np

import concourse.bass as bass
from concourse import mybir

F32 = mybir.dt.float32
F32R = mybir.dt.float32r
ALU = mybir.AluOpType
ACT = mybir.ActivationFunctionType
AX = mybir.AxisListType

P = 128
B, H, W, C = 8, 256, 256, 64
J = W // P
JC = J * C
HALF = H // P
KX = 32
RI = 2
PIX = H * W
EPS = 1e-5

ROWS = 16
CHUNKS = H // ROWS
UNIT = CHUNKS // HALF
NCH = B * CHUNKS
PAIR = 2
BROWS = 4
BANKS = ROWS // BROWS
NB = BROWS * JC
SLOTS = 4
GC = 4


class Layer:

    def __init__(self, ky, groups):
        self.KY = ky
        self.KYR = 2 * ky
        self.NG = groups
        self.GP = P // groups
        self.LO = self.GP
        self.K = self.LO + self.KYR
        self.M = KX * ky
        self.NQ = self.M // 2 // 8
        self.RM = 4
        self.R = self.M // (2 * 4 * self.RM)
        self.RR = C // (groups * GC)
        self.pieces = [(a, min(a + 8, ky)) for a in range(0, ky, 8)] if ky % 8 == 0 else [(0, 6), (6, 12), (12, 17)]


L0 = Layer(16, 4)
L1 = Layer(17, 2)


def tables():
    out = {"ident": np.eye(P)}
    kx = np.concatenate([np.arange(16), np.arange(-16, 0)])
    h = np.arange(H)
    ph = 2 * np.pi * ((kx[None, :] * h[:, None]) % H) / H
    c, s = np.cos(ph), np.sin(ph)
    fh = np.stack([np.concatenate([c, -s], 1), np.concatenate([-s, -c], 1)], 1)
    out["fwd_h"] = fh.reshape(P, PAIR * 2 * 2 * KX)
    out["inv_h"] = np.concatenate([c, -s], 1).T
    w = (J * np.arange(P)[None, :] + np.arange(J)[:, None])
    for n, lay in enumerate((L0, L1)):
        ky = np.arange(lay.KY)
        pw = 2 * np.pi * ((ky[None, None] * w[..., None]) % W) / W
        f = np.concatenate([np.cos(pw), np.sin(pw)], -1)
        out[f"fwd_w{n}"] = f.transpose(1, 0, 2).reshape(P, -1)
        m = np.tile(np.where(ky == 0, 1.0, 2.0), 2) / PIX
        g = (f * m).transpose(2, 0, 1)
        k = np.zeros((lay.K, J, P))
        k[:lay.KYR] = g
        k[lay.LO:] = g
        out[f"inv_w{n}"] = (k if n else np.concatenate([k, k])).reshape(-1, J * P)
    pair = np.arange(P) // 2
    out["pairs"] = (pair[:C, None] == (np.arange(P) % C // 2)[None, :]).astype(float)
    out["ones"] = np.ones((P, 8))
    return {k: np.ascontiguousarray(v, np.float32) for k, v in out.items()}


class Tiles:

    def __init__(self, nc, tag):
        self.nc, self.tag, self.stack = nc, tag, ExitStack()

    def __enter__(self):
        return self

    def __exit__(self, *a):
        return self.stack.__exit__(*a)

    def sb(self, name, shape, dt=F32):
        return self.stack.enter_context(self.nc.sbuf_tensor(f"{self.tag}_{name}", shape, dt))

    def ps(self, name, shape):
        return self.stack.enter_context(self.nc.psum_tensor(f"{self.tag}_{name}", shape, F32))

    def sem(self, name):
        return self.stack.enter_context(self.nc.semaphore(f"{self.tag}_{name}"))

    def sems(self, name, n):
        return [self.sem(f"{name}{i}") for i in range(n)]


def settle(eng, sem):
    eng.sem_inc(sem, 1)


def load_rows(eng, dst, src, sem):
    for h in range(0, ROWS, ROWS // 2):
        eng.dma_start(dst[:, h:h + ROWS // 2], src[:, h:h + ROWS // 2]).then_inc(sem, 16)


LOADED = 32


def load_constants(nc, d, k):
    with Tiles(nc, "c") as t:
        loaded, hi_done, split = t.sem("loaded"), t.sem("hi_done"), t.sem("split")
        raw = {0: t.sb("raw0", [P, J * P]), 1: t.sb("raw1", [L1.K, J * P])}
        hi0 = t.sb("hi0", [P, J * P], F32R)
        pairs = [(k["ident"], d["ident"]), (k["fwd_h"], d["fwd_h"]), (k["inv_h"], d["inv_h"]),
                 (k["fwd_w0"], d["fwd_w0"]), (k["fwd_w1"], d["fwd_w1"]), (k["pairs"], d["pairs"]),
                 (k["ones"], d["ones"]), (raw[0], d["inv_w0"]), (raw[1], d["inv_w1"])]
        with nc.Block() as block:
            @block.sync
            def _(sp):
                for dst, src in pairs:
                    sp.dma_start(dst[:], src).then_inc(loaded, 16)
                sp.wait_ge(hi_done, 1)
                for j in range(J):
                    sp.dma_start(k["wdiag"][j * C:(j + 1) * C, j * C:(j + 1) * C], d["W_res"]).then_inc(loaded, 16)
                sp.dma_start(k["wres"][:], d["W_res"]).then_inc(loaded, 16)
                sp.dma_start(k["bias"][:], d["b_res"].rearrange("(a c) -> a c", a=1).broadcast_to([B, C])).then_inc(loaded, 16)
                sp.wait_ge(loaded, 16 * (len(pairs) + J + 2))

            @block.vector
            def _(dve):
                nc.vector.memset(k["wdiag"][:], 0.0).then_inc(hi_done, 1)
                dve.wait_ge(loaded, 16 * (len(pairs) + J + 2))
                nc.vector.tensor_copy(hi0[:], raw[0][:]).then_inc(hi_done, 1)
                nc.vector.tensor_copy(k["inv_w1h"][:], raw[1][:]).then_inc(hi_done, 1)
                dve.wait_ge(hi_done, 3)
                nc.vector.tensor_copy(k["inv_w0"][0:C], raw[0][0:C]).then_inc(split, 1)
                nc.vector.tensor_tensor(k["inv_w0"][C:P], raw[0][C:P], hi0[C:P].bitcast(F32), ALU.subtract).then_inc(split, 1)
                nc.vector.tensor_tensor(k["inv_w1l"][:], raw[1][:], k["inv_w1h"][:].bitcast(F32), ALU.subtract).then_inc(split, 1)


def forward_w0(nc, lay, k, x_dram, t_dram, sq, wt):
    with Tiles(nc, "a") as t:
        x = t.sb("x", [P, SLOTS, ROWS, JC])
        q = t.sb("q", [P, 2, ROWS, JC])
        part = t.sb("part", [P, UNIT, C])
        ts = t.sb("ts", [P, 2, 512])
        tp = t.ps("tp", [P, 2, 512])
        loaded, stored = t.sems("loaded", SLOTS), t.sems("stored", 2)
        names = ("summed", "copied", "squared", "reduced", "final", "tick")
        summed, copied, squared, reduced, final, tick = (t.sem(n) for n in names)
        PAIRS = SLOTS // 2
        N = NCH // SLOTS
        with nc.Block() as block:
            @block.sync
            def _(sp):
                with sp.Fori(0, N) as i:
                    for s in range(SLOTS):
                        if s % 2 == 0:
                            sp.wait_ge(summed, PAIRS * i + s // 2 + 1)
                            settle(sp, tick)
                            sp.wait_ge(squared, SLOTS * i + s + 2)
                        load_rows(sp, x[:, s], x_dram[SLOTS * i + s], loaded[s])

            @block.tensor
            def _(pe):
                pe.sem_inc(summed, PAIRS)
                with pe.Fori(0, N) as i:
                    for r in range(PAIRS):
                        for s in (2 * r, 2 * r + 1):
                            pe.wait_ge(loaded[s], LOADED * (i + 1))
                        pe.wait_ge(copied, PAIRS * i + r + 1)
                        for j in range(J):
                            for g in range(4):
                                s, h = 2 * r + g // 2, 8 * (g % 2)
                                mm = nc.tensor.matmul(tp[32 * g:32 * g + lay.KYR, r], k["fwd_w0"][:, j * lay.KYR:(j + 1) * lay.KYR],
                                                      x[:, s, h:h + 8, j * C:(j + 1) * C], start=(j == 0), stop=(j == J - 1))
                        mm.then_inc(summed, 1)

            @block.scalar
            def _(act):
                act.sem_inc(copied, PAIRS)
                act.sem_inc(squared, SLOTS)
                for r in range(PAIRS):
                    act.sem_inc(stored[r], 64)
                wt.load(act, 0)

                def store_t(i, r):
                    act.wait_ge(summed, PAIRS * i + r + 1 + PAIRS)
                    act.wait_ge(stored[r], 64 * (i + 1))
                    nc.scalar.activation(ts[:, r], tp[:, r], ACT.Copy).then_inc(copied, 1)
                    act.wait_ge(copied, PAIRS * i + r + 1 + PAIRS)
                    for g in range(4):
                        act.dma_start(t_dram[4 * (PAIRS * i + r) + g], ts[32 * g:32 * g + lay.KYR, r]).then_inc(stored[r], 16)

                def body(i, first):
                    for s in range(SLOTS):
                        act.wait_ge(loaded[s], LOADED * (i + 1))
                        act.wait_ge(reduced, SLOTS * i + s + 1)
                        nc.scalar.activation(q[:, s % 2], x[:, s], ACT.Square).then_inc(squared, 1)
                        if s == 2:
                            store_t(i, 0)
                        if s == 0 and not first:
                            store_t(i - 1, 1)

                body(0, True)
                with act.Fori(1, N) as i:
                    body(i, False)
                store_t(N - 1, 1)
                for r in range(PAIRS):
                    act.wait_ge(stored[r], 64 * (N + 1))

            @block.vector
            def _(dve):
                dve.sem_inc(reduced, 2)
                dve.sem_inc(final, 1)
                with dve.Fori(0, B * HALF) as u:
                    for s in range(UNIT):
                        dve.wait_ge(squared, UNIT * u + s + 1 + SLOTS)
                        if s == 0:
                            dve.wait_ge(final, u + 1)
                        nc.vector.tensor_reduce(part[:, s], q[:, s % 2].rearrange("p h (j c) -> p c h j", j=J),
                                                AX.XY, ALU.add).then_inc(reduced, 1)
                    dve.wait_ge(reduced, UNIT * (u + 1) + 2)
                    nc.vector.tensor_reduce(sq[:, u], part[:].rearrange("p n c -> p c n"), AX.X, ALU.add).then_inc(final, 1)


def forward_h(nc, lay, tag, k, t_dram, xh_dram):
    with Tiles(nc, tag) as t:
        u = t.sb("u", [P, 2, lay.KYR, PAIR, C])
        xs = t.sb("xs", [P, 2, lay.KY * C])
        NP = len(lay.pieces)
        ps = t.ps("ps", [P, 2, NP, 512])
        loaded, stored = t.sems("loaded", 2), t.sems("stored", 2)
        summed, copied = t.sem("summed"), t.sem("copied")
        PARTS = 4
        cuts = [lay.KYR * n // PARTS for n in range(PARTS + 1)]
        place = [slice(2 * KX * (n % 2), 2 * KX * (n % 2 + 1)) for n in range(NP)]
        with nc.Block() as block:
            @block.sync
            def _(sp):
                with sp.Fori(0, B // 2) as i:
                    for s in range(2):
                        sp.wait_ge(summed, 2 * i + s + 1)
                        for a, e in zip(cuts, cuts[1:]):
                            sp.dma_start(u[:, s, a:e].rearrange("p k e c -> p k (e c)"), t_dram[2 * i + s][:, a:e]).then_inc(loaded[s], 16)

            @block.tensor
            def _(pe):
                pe.sem_inc(summed, 2)
                with pe.Fori(0, B // 2) as i:
                    for s in range(2):
                        pe.wait_ge(loaded[s], 16 * PARTS * (i + 1))
                        pe.wait_ge(copied, 2 * i + s + 1)
                        for first in range(0, NP, 2):
                            for e in range(PAIR):
                                for cs in range(2):
                                    tab = k["fwd_h"][:, (e * 2 + cs) * 2 * KX:(e * 2 + cs + 1) * 2 * KX]
                                    for n in range(first, min(first + 2, NP)):
                                        a, b = lay.pieces[n]
                                        mm = nc.tensor.matmul(ps[place[n], s, n, 0:(b - a) * C], tab,
                                                              u[:, s, cs * lay.KY + a:cs * lay.KY + b, e],
                                                              start=(e == 0 and cs == 0), stop=(e == PAIR - 1 and cs == 1))
                        mm.then_inc(summed, 1)

            @block.scalar
            def _(act):
                act.sem_inc(copied, 2)
                for s in range(2):
                    act.sem_inc(stored[s], 16 * 2 * NP)
                with act.Fori(0, B // 2) as i:
                    for s in range(2):
                        act.wait_ge(summed, 2 * i + s + 1 + 2)
                        act.wait_ge(stored[s], 16 * 2 * NP * (i + 1))
                        for n, (a, e) in enumerate(lay.pieces):
                            last = nc.scalar.activation(xs[place[n], s, a * C:e * C], ps[place[n], s, n, 0:(e - a) * C], ACT.Copy)
                        last.then_inc(copied, 1)
                        act.wait_ge(copied, 2 * i + s + 1 + 2)
                        for n, (a, e) in enumerate(lay.pieces):
                            for ri in range(RI):
                                row = place[n].start + ri * KX
                                act.dma_start(xh_dram[:, ri, 2 * i + s, :, a * C:e * C],
                                              xs[row:row + KX, s, a * C:e * C]).then_inc(stored[s], 16)
                for s in range(2):
                    act.wait_ge(stored[s], 16 * 2 * NP * (B // 2 + 1))


def mix_modes(nc, lay, tag, k, sq, xh_dram, y_dram, wt):
    M, NQ, R, RM = lay.M, lay.NQ, lay.R, lay.RM
    Q2 = 2
    NT = NQ // Q2
    UR = wt.UNROLL
    LOOP = (R - 1) // UR
    YS = 4
    with Tiles(nc, tag) as t:
        xl = t.sb("xl", [P, 2, NQ * C])
        xt = t.sb("xt", [P, M // 2, RI, B])
        xr = t.sb("xr", [P, 2, 4, RM, 3, B])
        ys = t.sb("ys", [P, YS, 2, RM * C])
        st = t.sb("st", [P, 10, B])
        bt = t.sb("bt", [B, C])
        pt = t.ps("pt", [P, 2, 512])
        py = t.ps("py", [P, 2, 2, 512])
        names = ("xl", "statistic_mm", "statistic", "turned", "scaled", "dc", "staged", "mixed", "copied", "zeroed", "ready", "tick")
        S = {n: t.sem(n) for n in names}
        stored = t.sems("stored", YS)
        wt.begin(t, S)
        DC, SSQ, MEAN, EX2, MSQ, VAR, SD, SCALE, SHIFT, SHIFT_DC = range(10)
        with nc.Block() as block:
            def store_rounds(eng):
                def store(r, z):
                    eng.wait_ge(S["ready"], r + 2)
                    for g in range(4):
                        eng.dma_start(y_dram[g][r], ys[32 * g:32 * g + RI * B, z]).then_inc(stored[z], 16)

                with eng.Fori(0, R // YS) as i:
                    for z in range(YS):
                        store(YS * i + z, z)
                for r in range(R // YS * YS, R):
                    store(r, r % YS)
                for z in range(YS):
                    eng.wait_ge(stored[z], 16 * 4 * len(range(z, R, YS)))

            @block.sync
            def _(sp):
                for half in range(2):
                    sp.dma_start(xl[:, half], xh_dram[half]).then_inc(S["xl"], 16)
                wt.prefetch(sp)
                wt.sync(sp)
                if lay is L0:
                    store_rounds(sp)

            @block.gpsimd
            def _(pool):
                if lay is L1:
                    store_rounds(pool)

            @block.tensor
            def _(pe):
                pe.sem_inc(S["mixed"], 1)
                pe.wait_ge(S["xl"], 32)

                def turn(q):
                    for half in range(2):
                        tr = nc.tensor.matmul(pt[half * C:(half + 1) * C, (q // Q2) % 2, (q % Q2) * P:(q % Q2 + 1) * P],
                                              xl[:, half, q * C:(q + 1) * C], k["ident"][:], start=True, stop=True,
                                              skip_group_check=True)
                    return tr

                def mix_round(r, z):
                    wt.tensor(pe, r)
                    pe.wait_ge(S["staged"], r + 1)
                    pe.wait_ge(S["copied"], r + 1)
                    settle(pe, S["tick"])
                    for m in range(RM):
                        for part in range(2):
                            for g in range(4):
                                for half in range(2):
                                    rows = slice(half * C, half * C + C)
                                    out = py[32 * g:32 * g + RI * B, z, half, m * C:(m + 1) * C]
                                    lhs = xr[rows, z, g, m, 1 - part:3 - part]
                                    mm = nc.tensor.matmul(out, lhs, wt.rhs(half, g, m, part, z), start=(part == 0),
                                                          stop=(part == 1), skip_group_check=True)
                    mm.then_inc(S["mixed"], 1)

                pe.wait_ge(S["zeroed"], 1)
                for b in range(B):
                    for half in range(HALF):
                        nc.tensor.matmul(py[0:C, 0, 0, b:b + 1], sq[:, HALF * b + half], k["ones"][:, 0:1], start=(half == 0),
                                         stop=(half == HALF - 1), skip_group_check=True)
                for q in range(Q2):
                    turn(q).then_inc(S["turned"], 1)
                pe.wait_ge(S["statistic"], 2)
                nc.tensor.matmul(py[:, 1, 0, 0:2 * B], k["pairs"][:], st[0:C, DC:SSQ + 1], start=True, stop=True,
                                 skip_group_check=True).then_inc(S["statistic_mm"], 1)
                if lay is L0:
                    pe.wait_ge(S["statistic"], 9)
                    nc.tensor.matmul(py[0:B, 1, 0, 128:128 + C], st[0:C, SHIFT], k["wres"][:], start=True, stop=True,
                                     skip_group_check=True).then_inc(S["statistic_mm"], 1)
                for n in range(1, NT):
                    if n >= 2:
                        pe.wait_ge(S["scaled"], n - 1)
                    for q in range(Q2 * n, Q2 * n + Q2):
                        turn(q).then_inc(S["turned"], 1)
                wt.tensor_start(pe)
                with pe.Fori(0, LOOP) as i:
                    for z in range(UR):
                        wt.tensor_next(pe, UR * i + z + 1, (z + 1) % UR, i + (z + 1) // UR)
                        mix_round(UR * i + z, z % 2)
                for r in range(UR * LOOP, R):
                    if r + 1 < R:
                        wt.tensor_next(pe, r + 1, (r + 1) % UR, (r + 1) // UR)
                    mix_round(r, r % 2)

            @block.scalar
            def _(act):
                act.wait_ge(S["statistic"], 6)
                nc.scalar.activation(st[:, SD], st[:, VAR], ACT.Sqrt).then_inc(S["statistic"], 1)
                wt.scalar(act)

            @block.vector
            def _(dve):
                nc.vector.memset(py[:], 0.0).then_inc(S["zeroed"], 1)
                dve.sem_inc(S["ready"], 1)
                dve.sem_inc(S["copied"], 2)
                dve.wait_ge(S["turned"], Q2)
                first = pt[:, 0, 0:P].rearrange("p (r b m) -> p r b m", r=RI, b=B)
                nc.vector.tensor_copy(st[0:C, DC], first[0:C, 0, :, 0]).then_inc(S["statistic"], 1)
                nc.vector.tensor_copy(st[0:C, SSQ], py[0:C, 0, 0, 0:B]).then_inc(S["statistic"], 1)
                dve.wait_ge(S["statistic_mm"], 1)
                n = 1.0 / (2 * PIX)
                nc.vector.tensor_scalar(st[:, MEAN], py[:, 1, 0, 0:B], n, None, ALU.mult).then_inc(S["statistic"], 1)
                nc.vector.tensor_scalar(st[:, EX2], py[:, 1, 0, B:2 * B], n, EPS, ALU.mult, ALU.add).then_inc(S["statistic"], 1)
                dve.wait_ge(S["statistic"], 4)
                nc.vector.tensor_tensor(st[:, MSQ], st[:, MEAN], st[:, MEAN], ALU.mult).then_inc(S["statistic"], 1)
                dve.wait_ge(S["statistic"], 5)
                nc.vector.tensor_tensor(st[:, VAR], st[:, EX2], st[:, MSQ], ALU.subtract).then_inc(S["statistic"], 1)
                dve.wait_ge(S["statistic"], 7)
                nc.vector.reciprocal(st[:, SCALE], st[:, SD]).then_inc(S["statistic"], 1)
                dve.wait_ge(S["statistic"], 8)
                nc.vector.tensor_tensor(st[:, SHIFT], st[:, SCALE], st[:, MEAN], ALU.mult).then_inc(S["statistic"], 1)
                dve.wait_ge(S["statistic"], 9)
                nc.vector.tensor_scalar(st[:, SHIFT_DC], st[:, SHIFT], float(PIX), None, ALU.mult).then_inc(S["statistic"], 1)

                scale = st[:, SCALE].rearrange("p (a b) -> p a b", a=1).broadcast_to([P, 8, B])
                by_q = xt[:].rearrange("p (m q) r b -> p q r m b", m=8)
                for n in range(NT):
                    dve.wait_ge(S["turned"], Q2 * (n + 1))
                    for q in range(Q2):
                        for ri in range(RI):
                            src = pt[:, n % 2, q * P:(q + 1) * P].rearrange("p (r b m) -> p r m b", r=RI, b=B)[:, ri]
                            last = nc.vector.tensor_tensor(by_q[:, Q2 * n + q, ri], src, scale, ALU.mult)
                    last.then_inc(S["scaled"], 1)
                dve.wait_ge(S["scaled"], NT)
                dve.wait_ge(S["statistic"], 10)
                nc.vector.tensor_tensor(xt[0:C, 0, 0], xt[0:C, 0, 0], st[0:C, SHIFT_DC], ALU.subtract).then_inc(S["dc"], 1)
                if lay is L0:
                    dve.wait_ge(S["statistic_mm"], 2)
                    nc.vector.tensor_tensor(bt[:], k["bias"][:], py[0:B, 1, 0, 128:128 + C], ALU.subtract).then_inc(S["dc"], 1)
                    for b in range(B):
                        nc.vector.tensor_scalar(k["wscaled"][:, b], k["wdiag"][:], st[:, SCALE, b:b + 1], None,
                                                ALU.mult).then_inc(S["dc"], 1)
                    dve.wait_ge(S["dc"], B + 2)
                else:
                    dve.wait_ge(S["dc"], 1)
                by_round = xt[:].rearrange("p (r g m) s b -> p r g m (s b)", g=4, r=R)

                def stage(r, z):
                    for m in range(RM):
                        nc.vector.tensor_copy(xr[:, z, :, m, 1:3].rearrange("p g s b -> p g (s b)"), by_round[:, r, :, m])
                        last = nc.vector.tensor_scalar(xr[:, z, :, m, 0], by_round[:, r, :, m, B:2 * B], -1.0, None, ALU.mult)
                    last.then_inc(S["staged"], 1)

                def copy_out(r, z, y, n):
                    dve.wait_ge(S["mixed"], r + 2)
                    dve.wait_ge(stored[y], 16 * 4 * n)
                    cp = nc.vector.tensor_copy(ys[:, y], py[:, z, :, 0:RM * C])
                    cp.then_inc(S["copied"], 1)
                    if lay is L0 and isinstance(r, int) and r == 0:
                        dve.wait_ge(S["copied"], 3)
                        cp = nc.vector.scalar_tensor_tensor(out=ys[0:B, 0, 0, 0:C], in0=bt[:], scalar=float(PIX),
                                                            in1=ys[0:B, 0, 0, 0:C], op0=ALU.mult, op1=ALU.add)
                        cp.then_inc(S["ready"], 1)
                    else:
                        dve.wait_ge(S["copied"], r + 3)
                        dve.sem_inc(S["ready"], 1)

                def round_(r, z, y, n):
                    if not (isinstance(r, int) and r + 1 >= R):
                        dve.wait_ge(S["mixed"], r + 1)
                        stage(r + 1, 1 - z)
                    copy_out(r, z, y, n)

                stage(0, 0)
                for r in range(YS):
                    round_(r, r % 2, r, 0)
                FULL = (R - 1) // YS
                with dve.Fori(1, FULL) as i:
                    for y in range(YS):
                        round_(YS * i + y, y % 2, y, i)
                for r in range(YS * FULL, R):
                    round_(r, r % 2, r % YS, r // YS)


class Weights0:
    UNROLL = 4
    PARTS = 2

    def __init__(self, nc, lay, t, weights_dram):
        self.nc, self.lay, self.dram = nc, lay, weights_dram
        self.raw = t.sb("raw", [P, self.PARTS, C, lay.M // 2 * RI // self.PARTS])
        self.loaded = t.sems("loaded", self.PARTS)

    def load(self, eng, part):
        for half in range(2):
            for o in range(0, C, C // 4):
                cols = slice(o, o + C // 4)
                eng.dma_start(self.raw[half * C:(half + 1) * C, part, cols],
                              self.dram[half][part][:, cols]).then_inc(self.loaded[part], 16)

    def prefetch(self, sp):
        self.load(sp, 1)

    def begin(self, t, S):
        self.S = S
        self.w = t.sb("w", [P, 2, 4 * self.lay.RM, RI * C])
        self.packed = t.sem("w_packed")

    def sync(self, sp):
        pass

    def tensor_start(self, pe):
        pass

    def tensor_next(self, pe, r, slot, n):
        pass

    def tensor(self, pe, r):
        pe.wait_ge(self.packed, r + 1)

    def scalar(self, act):
        rounds = self.lay.R // self.PARTS
        for part in range(self.PARTS):
            act.wait_ge(self.loaded[part], 16 * 8)
            by_round = self.raw[:, part].rearrange("p o (r x) -> p r x o", r=rounds)
            with act.Fori(0, rounds // 2) as i:
                for z in range(2):
                    act.wait_ge(self.S["mixed"], rounds * part + 2 * i + z)
                    dst = self.w[:, z].rearrange("p q (i o) -> p (q i) o", i=RI)
                    self.nc.scalar.activation(dst, by_round[:, 2 * i + z], ACT.Copy).then_inc(self.packed, 1)

    def rhs(self, half, g, m, part, z):
        return self.w[half * C:half * C + C, z, g * self.lay.RM + m, part * C:part * C + C]


class Weights1:
    UNROLL = 8

    def __init__(self, nc, lay, t, k, weights_dram):
        self.nc, self.lay, self.k, self.dram = nc, lay, k, weights_dram
        self.raw = t.sb("raw", [P, self.UNROLL, 4 * lay.RM, 2, C])
        self.loaded = t.sems("loaded", self.UNROLL)

    def load(self, eng, r, slot):
        for ri in range(RI):
            for half in range(2):
                eng.dma_start(self.raw[ri * C:(ri + 1) * C, slot, :, half], self.dram[ri][half][r]).then_inc(self.loaded[slot], 16)

    def prefetch(self, sp):
        for r in range(self.UNROLL):
            self.load(sp, r, r)

    def begin(self, t, S):
        self.S = S
        self.w = t.sb("w", [P, 2, 4 * self.lay.RM, P])
        self.ps = t.ps("pw", [P, 2, 512])
        self.turned, self.copied = t.sem("w_turned"), t.sem("w_copied")

    def sync(self, sp):
        U, R = self.UNROLL, self.lay.R

        def reload(r, slot):
            sp.wait_ge(self.turned, 4 * (r - U) + 8)
            self.load(sp, r, slot)

        with sp.Fori(1, R // U) as i:
            for z in range(U):
                reload(U * i + z, z)
        for r in range(R // U * U, R):
            reload(r, r % U)

    def tensor_start(self, pe):
        pe.sem_inc(self.turned, 4)
        self.tensor_next(pe, 0, 0, 0)

    def tensor_next(self, pe, r, slot, n):
        pe.wait_ge(self.loaded[slot], 64 * (n + 1))
        for b in range(4):
            pe.wait_ge(self.copied, 4 * r + b + 1)
            for q in range(4 * b, 4 * b + 4):
                mm = self.nc.tensor.transpose(self.ps[:, b % 2, (q % 4) * P:(q % 4 + 1) * P],
                                              self.raw[:, slot, q].rearrange("p a c -> p (a c)"), self.k["ident"][:])
            mm.then_inc(self.turned, 1)

    def tensor(self, pe, r):
        pe.wait_ge(self.copied, 4 * r + 6)

    def scalar(self, act):
        act.sem_inc(self.copied, 2)

        def body(r, z):
            act.wait_ge(self.S["mixed"], r)
            for b in range(4):
                act.wait_ge(self.turned, 4 * r + b + 5)
                self.nc.scalar.activation(self.w[:, z, 4 * b:4 * b + 4].rearrange("p q c -> p (q c)"), self.ps[:, b % 2],
                                          ACT.Copy).then_inc(self.copied, 1)
        with act.Fori(0, self.lay.R // 2) as i:
            for z in range(2):
                body(2 * i + z, z)
        body(self.lay.R - 1, 0)

    def rhs(self, half, g, m, part, z):
        return self.w[half * C:half * C + C, z, g * self.lay.RM + m, part * C:part * C + C]


class InverseH:

    def __init__(self, nc, lay, t, k, y_dram, spare, banks):
        self.nc, self.lay, self.k, self.y_dram = nc, lay, k, y_dram
        self.y = t.sb("y", [RI * KX, lay.GP, C])
        self.g = t.sb("g", [P, 2, P, C], F32R)
        self.tab = t.sb("tab", [RI * KX, P])
        self.banks = banks
        self.ps = t.ps("pg", [P, banks, 512])
        self.ahead = lay.NG * (banks - 1)
        self.first = spare + [self.ps[:, n] for n in range(banks)]
        self.loaded, self.ready = t.sem("y_loaded"), t.sem("y_ready")
        self.summed, self.hi, self.lo = (t.sem("g_" + n) for n in ("summed", "hi", "lo"))
        self.doubled = t.sems("g_doubled", 2)
        self.tick, self.tick_sp = t.sem("g_tick"), t.sem("g_tick_sp")

    def load(self, sp, b):
        sp.wait_ge(self.summed, self.lay.RR * HALF * b + 1)
        settle(sp, self.tick_sp)
        sp.wait_ge(self.ready, 3 * b + 1)
        for cs in range(2):
            for ri in range(RI):
                src = self.y_dram[ri if cs == 0 else 1 - ri][b]
                rows = slice(cs * self.lay.KY, (cs + 1) * self.lay.KY)
                sp.dma_start(self.y[ri * KX:(ri + 1) * KX, rows].rearrange("p k c -> p (k c)"), src).then_inc(self.loaded, 16)

    def start_tensor(self, pe):
        pe.sem_inc(self.summed, 1)
        for r in range(self.lay.RR):
            self.tensor(pe, r, 0, 0, True)

    def start_scalar(self, act):
        for r in range(self.lay.RR):
            for g in range(self.lay.NG):
                self.high(act, r, g, 0, 0, True)

    def start_vector(self, dve):
        dve.sem_inc(self.lo, self.ahead + 1)
        if self.lay.GP > self.lay.KYR:
            self.nc.vector.memset(self.y[:, self.lay.KYR:], 0.0).then_inc(self.ready, 1)
        else:
            dve.sem_inc(self.ready, 1)
        self.prepare(dve, 0, 0)
        for r in range(self.lay.RR):
            for g in range(self.lay.NG):
                self.low(dve, r, g, 0, 0, True)

    def rounds(self, b, half):
        return self.lay.RR * (HALF * b + half)

    def prepare(self, dve, b, half):
        dve.wait_ge(self.summed, self.rounds(b, half) + 1)
        self.nc.vector.tensor_copy(self.tab[:], self.k["inv_h"][:, half * P:(half + 1) * P]).then_inc(self.ready, 1)
        if half == 0:
            dve.wait_ge(self.loaded, 64 * (b + 1))
            iy = self.y[0:KX, self.lay.KY:self.lay.KYR]
            self.nc.vector.tensor_scalar(iy, iy, -1.0, None, ALU.mult).then_inc(self.ready, 1)

    def bank(self, r, first):
        return self.first[r % len(self.first)] if first else self.ps[:, r % self.banks]

    def tensor(self, pe, r, b, half, first=False):
        lay = self.lay
        pe.wait_ge(self.ready, 3 * b + 3 + half)
        if not first:
            pe.wait_ge(self.lo, lay.NG * (self.rounds(b, half) + r) + 1)
        settle(pe, self.tick)
        for cc in range(GC):
            for g in range(lay.NG):
                c = (g * lay.RR + r) * GC + cc
                mm = self.nc.tensor.matmul(self.bank(r, first)[lay.GP * g:lay.GP * (g + 1), cc * P:(cc + 1) * P],
                                           self.y[:, :, c], self.tab[:],
                                           start=True, stop=True, skip_group_check=True)
        mm.then_inc(self.summed, 1)

    def piece(self, r, g, first, count):
        lay = self.lay
        c = (g * lay.RR + r) * GC
        rows = self.bank(r, first)[lay.GP * g:lay.GP * g + count]
        return rows.rearrange("p (c h) -> p h c", h=P), slice(c, c + GC)

    def high(self, act, r, g, b, half, first=False):
        lay = self.lay
        if g == 0:
            act.wait_ge(self.summed, self.rounds(b, half) + r + 2)
        src, cols = self.piece(r, g, first, lay.GP)
        self.nc.scalar.activation(self.g[0:lay.GP, half, :, cols], src, ACT.Copy).then_inc(self.hi, 1)

    def low(self, dve, r, g, b, half, first=False):
        lay = self.lay
        dve.wait_ge(self.hi, lay.NG * (self.rounds(b, half) + r) + g + 1)
        src, cols = self.piece(r, g, first, lay.KYR)
        self.nc.vector.tensor_tensor(self.g[lay.LO:lay.LO + lay.KYR, half, :, cols], src,
                                     self.g[0:lay.KYR, half, :, cols].bitcast(F32), ALU.subtract).then_inc(self.lo, 1)

    def complete(self, eng, b, half):
        eng.wait_ge(self.lo, self.lay.NG * (self.rounds(b, half) + self.lay.RR) + self.ahead + 1)

    def double(self, sp, b, half):
        self.complete(sp, b, half)
        rows = 2 * self.lay.LO
        sp.dma_start(self.g[rows:2 * rows, half].rearrange("p h c -> p (h c)").bitcast(F32),
                     self.g[0:rows, half].rearrange("p h c -> p (h c)").bitcast(F32)).then_inc(self.doubled[half], 16)

    def inverse_w1(self, tab, z, slot, row):
        out = z.rearrange("p (h j c) -> p j h c", j=J, c=C)
        for j in range(J):
            mm = self.nc.tensor.matmul(out[:, j], tab[:, j * P:(j + 1) * P], self.g[:, slot, row:row + BROWS],
                                       start=(j == 0), stop=True, skip_group_check=True)
        return mm

    def inverse_w(self, tables, z, slot, row):
        lay = self.lay
        out = z.rearrange("p (h j c) -> p j h c", j=J, c=C)
        for n, tab in enumerate(tables):
            for j in range(J):
                mm = self.nc.tensor.matmul(out[:, j], tab[:, j * P:(j + 1) * P], self.g[0:lay.K, slot, row:row + BROWS],
                                           start=(n == 0 and j == 0), stop=(n == 1), skip_group_check=True)
        return mm


def pixels0(nc, lay, k, x_dram, y_dram, x1_dram, t_dram, sq):
    NU = B * HALF
    STEPS = UNIT * BANKS
    HR = ROWS // 2
    with Tiles(nc, "b") as t:
        x = t.sb("x", [P, SLOTS, ROWS, JC])
        x1 = t.sb("x1", [P, SLOTS, ROWS, JC])
        xt = t.sb("xt", [P, 2, NB])
        q = t.sb("q", [P, 2, HR, JC])
        part = t.sb("part", [P, 2 * UNIT, C])
        ts = t.sb("ts", [P, 2, 512])
        pt = t.ps("pt", [P, 2, NB])
        z = t.ps("z", [P, BANKS, NB])
        tp = t.ps("tp", [P, 512])
        G = InverseH(nc, lay, t, k, y_dram, [z[:, m] for m in range(BANKS)], 1)
        loaded, x1_stored, t_stored = t.sems("loaded", SLOTS), t.sems("x1_stored", SLOTS), t.sems("t_stored", 2)
        names = ("turned", "turned_copied", "pixels", "silu", "added", "summed", "t_copied", "squared", "reduced", "final")
        turned, turned_copied, pixels, silu, added, summed, t_copied, squared, reduced, final = (t.sem(n) for n in names)
        APART = lay.NG + 2
        sums_at = {2 + APART * r: r for r in range(lay.RR)}
        high_at = {2 + APART * r + 1 + g: (r, g) for r in range(lay.RR) for g in range(lay.NG)}
        low_at = {2 + APART * r + 4 + g: (r, g) for r in range(lay.RR) for g in range(lay.NG)}
        AFTER = {"forward": 6, "square0": 4, "square1": 6, "t_copy": 7, "reduce0": 7, "reduce1": 9}
        DOUBLE_AT = UNIT - 1
        assert max(low_at) < BANKS * DOUBLE_AT

        def units(eng, body):
            body(0, 0, 0, True, False)
            with eng.Fori(0, B - 1) as i:
                body(i, 1, i + 1, False, False)
                body(i + 1, 0, i + 1, False, False)
            body(B - 1, 1, None, False, True)

        def due(kinds, step, first=False):
            for kind in kinds:
                s, rest = divmod(step - AFTER[kind], BANKS)
                if rest == 0 and s < UNIT and not (first and s < 0):
                    yield kind, s

        TAIL = range(STEPS, STEPS + 2 * BANKS + 2)

        with nc.Block() as block:
            @block.sync
            def _(sp):
                for s in range(SLOTS):
                    sp.sem_inc(x1_stored[s], 16)
                for s in range(2):
                    sp.sem_inc(t_stored[s], 32)

                def x1_store(n, s):
                    sp.wait_ge(added, 2 * (n + 1))
                    sp.dma_start(x1_dram[n], x1[:, s % SLOTS].rearrange("p h c -> p (h c)")).then_inc(x1_stored[s % SLOTS], 16)

                def t_store(n, s):
                    sp.wait_ge(t_copied, n + 2)
                    for g in range(2):
                        sp.dma_start(t_dram[2 * n + g], ts[C * g:C * g + L1.KYR, s % 2]).then_inc(t_stored[s % 2], 16)

                def unit(b, half, after, first, last, Y=None):
                    u = HALF * b + half
                    for s in range(UNIT):
                        n = UNIT * u + s
                        if s == DOUBLE_AT - 1 and Y is not None:
                            G.load(sp, Y)
                        if s == DOUBLE_AT and not last:
                            G.double(sp, after, 1 - half)
                        if not (first and s == 0):
                            sp.wait_ge(added, 2 * n)
                        if not (last and s + 3 >= UNIT):
                            load_rows(sp, x[:, (s + 3) % SLOTS], x_dram[n + 3], loaded[(s + 3) % SLOTS])
                        if not (first and s < 1):
                            x1_store(n - 1, s + SLOTS - 1)
                        if not (first and s < 2):
                            t_store(n - 2, s)

                G.load(sp, 0)
                for s in range(SLOTS - 1):
                    load_rows(sp, x[:, s], x_dram[s], loaded[s])
                G.double(sp, 0, 0)
                unit(0, 0, 0, True, False, 1)
                with sp.Fori(0, B - 2) as i:
                    unit(i, 1, i + 1, False, False)
                    unit(i + 1, 0, i + 1, False, False, i + 2)
                unit(B - 2, 1, B - 1, False, False)
                unit(B - 1, 0, B - 1, False, False)
                unit(B - 1, 1, None, False, True)
                x1_store(NCH - 1, SLOTS - 1)
                t_store(NCH - 2, 0)
                t_store(NCH - 1, 1)
                for s in range(SLOTS):
                    sp.wait_ge(x1_stored[s], 16 * (NCH // SLOTS + 1))
                for s in range(2):
                    sp.wait_ge(t_stored[s], 32 * (NCH // 2 + 1))

            @block.tensor
            def _(pe):
                pe.sem_inc(summed, SLOTS)
                G.start_tensor(pe)

                def turn(u, i):
                    s, m = i // BANKS, i % BANKS
                    if m == 0:
                        pe.wait_ge(loaded[s % SLOTS], LOADED * (2 * u + s // SLOTS + 1))
                    for h in range(BROWS):
                        tr = nc.tensor.transpose(pt[:, m % 2, h * P:(h + 1) * P], x[:, s % SLOTS, BROWS * m + h], k["ident"][:])
                    tr.then_inc(turned, 1)

                def forward(u, s):
                    n = UNIT * u + s
                    pe.wait_ge(added, 2 * n + 2)
                    pe.wait_ge(t_copied, n + 1)
                    for j in range(J):
                        for g in range(2):
                            mm = nc.tensor.matmul(tp[C * g:C * g + L1.KYR], k["fwd_w1"][:, j * L1.KYR:(j + 1) * L1.KYR],
                                                  x1[:, s % SLOTS, 8 * g:8 * g + 8, j * C:(j + 1) * C], start=(j == 0), stop=(j == J - 1))
                    mm.then_inc(summed, 1)

                def body(b, half, after, first, last):
                    u = HALF * b + half
                    pe.wait_ge(G.doubled[half], 16 * (b + 1))
                    for i in range(STEPS):
                        s, m = i // BANKS, i % BANKS
                        bank = STEPS * u + i
                        if not (last and i + 1 == STEPS):
                            turn(u + (i + 1) // STEPS, (i + 1) % STEPS)
                        pe.wait_ge(silu, bank + 1)
                        G.inverse_w1(k["inv_w0"], z[:, m], half, ROWS * s + BROWS * m)
                        pe.wait_ge(turned_copied, bank + 1)
                        for h in range(BROWS):
                            cols = slice(h * P, (h + 1) * P)
                            mm = nc.tensor.matmul(z[:, m, cols], xt[:, m % 2, cols], k["wscaled"][:, b],
                                                  start=False, stop=True, skip_group_check=True)
                        mm.then_inc(pixels, 1)
                        for _, c in due(["forward"], i, first):
                            forward(u, c)
                        if i in sums_at and not last:
                            G.tensor(pe, sums_at[i], after, 1 - half)

                turn(0, 0)
                units(pe, body)
                for i in TAIL:
                    for _, c in due(["forward"], i):
                        forward(NU - 1, c)

            @block.scalar
            def _(act):
                act.sem_inc(silu, BANKS)
                act.sem_inc(t_copied, 1)
                act.sem_inc(squared, 2 * SLOTS)
                G.start_scalar(act)

                def square(u, s, half):
                    n = 2 * (UNIT * u + s) + half
                    act.wait_ge(added, n + 1)
                    act.wait_ge(reduced, n + 1)
                    nc.scalar.activation(q[:, half], x1[:, s % SLOTS, HR * half:HR * (half + 1)], ACT.Square).then_inc(squared, 1)

                def t_copy(u, s):
                    act.wait_ge(summed, UNIT * u + s + 1 + SLOTS)
                    act.wait_ge(t_stored[s % 2], 32 * (UNIT // 2) * u + 32 * (s // 2) + 32)
                    for g in range(2):
                        rows = slice(C * g, C * g + L1.KYR)
                        last = nc.scalar.activation(ts[rows, s % 2], tp[rows], ACT.Copy)
                    last.then_inc(t_copied, 1)

                def x1_work(u, i, first):
                    for kind, c in due(["square0", "square1", "t_copy"], i, first):
                        t_copy(u, c) if kind == "t_copy" else square(u, c, int(kind[-1]))

                def body(b, half, after, first, last):
                    u = HALF * b + half
                    for i in range(STEPS):
                        s, m = i // BANKS, i % BANKS
                        n = UNIT * u + s
                        act.wait_ge(pixels, STEPS * u + i + 1)
                        if m == 0:
                            act.wait_ge(summed, n + 1)
                            act.wait_ge(squared, 2 * n + 2)
                            act.wait_ge(x1_stored[s % SLOTS], 32 * u + 16 * (s // SLOTS) + 16)
                        nc.scalar.activation(x1[:, s % SLOTS, BROWS * m:BROWS * (m + 1)].rearrange("p h c -> p (h c)"),
                                             z[:, m], ACT.Silu).then_inc(silu, 1)
                        if i in high_at and not last:
                            G.high(act, *high_at[i], after, 1 - half)
                        x1_work(u, i, first)

                units(act, body)
                for i in TAIL:
                    x1_work(NU - 1, i, False)

            @block.gpsimd
            def _(pool):
                with pool.Fori(0, NU) as u:
                    for s in range(UNIT):
                        for half in range(2):
                            rows = slice(HR * half, HR * (half + 1))
                            pool.wait_ge(silu, BANKS * (UNIT * u + s + 1) + 2 * (half + 1))
                            nc.gpsimd.tensor_tensor(x1[:, s % SLOTS, rows], x1[:, s % SLOTS, rows], x[:, s % SLOTS, rows],
                                                    ALU.add).then_inc(added, 1)

            @block.vector
            def _(dve):
                dve.sem_inc(reduced, 2)
                dve.sem_inc(final, 1)
                G.start_vector(dve)

                def reduce(u, s, half):
                    if s == 0 and half == 0:
                        dve.wait_ge(final, u + 1)
                    dve.wait_ge(squared, 2 * (UNIT * u + s) + half + 1 + 2 * SLOTS)
                    nc.vector.tensor_reduce(part[:, 2 * (s % UNIT) + half], q[:, half].rearrange("p h (j c) -> p c h j", j=J),
                                            AX.XY, ALU.add).then_inc(reduced, 1)

                def x1_work(u, i, first):
                    for kind, c in due(["reduce0", "reduce1"], i, first):
                        reduce(u, c, int(kind[-1]))
                        if kind == "reduce1" and c % UNIT == UNIT - 1:
                            v = u + c // UNIT
                            dve.wait_ge(reduced, 2 * UNIT * (v + 1) + 2)
                            nc.vector.tensor_reduce(sq[:, v], part[:].rearrange("p n c -> p c n"), AX.X, ALU.add).then_inc(final, 1)

                def body(b, half, after, first, last):
                    u = HALF * b + half
                    for i in range(STEPS):
                        s, m = i // BANKS, i % BANKS
                        dve.wait_ge(turned, STEPS * u + i + 1)
                        nc.vector.tensor_copy(xt[:, m % 2], pt[:, m % 2]).then_inc(turned_copied, 1)
                        if i == 0 and not last:
                            G.prepare(dve, after, 1 - half)
                        if i in low_at and not last:
                            G.low(dve, *low_at[i], after, 1 - half)
                        x1_work(u, i, first)

                units(dve, body)
                for i in TAIL:
                    x1_work(NU - 1, i, False)


def pixels1(nc, lay, k, x1_dram, y_dram, out_dram):
    DEEP = UNIT
    with Tiles(nc, "p") as t:
        x = t.sb("x", [P, DEEP, ROWS, JC])
        z = t.ps("z", [P, 4, NB])
        G = InverseH(nc, lay, t, k, y_dram, [z[:, m] for m in range(4)], 4)
        loaded, stored = t.sems("loaded", DEEP), t.sems("stored", DEEP)
        spectral, added = t.sem("spectral"), t.sem("added")
        tabs = (k["inv_w1h"], k["inv_w1l"])
        NU = B * HALF
        STEPS = UNIT * BANKS
        APART = lay.NG + 1
        sums_at = {1 + APART * r: r for r in range(lay.RR)}
        high_at = {1 + APART * r + g: (r, g) for r in range(lay.RR) for g in range(lay.NG)}
        low_at = {2 + APART * r + g: (r, g) for r in range(lay.RR) for g in range(lay.NG)}
        assert max(low_at) < STEPS

        def units(eng, body):
            body(0, 0, 0, False)
            with eng.Fori(0, B - 1) as i:
                body(i, 1, i + 1, False)
                body(i + 1, 0, i + 1, False)
            body(B - 1, 1, None, True)

        with nc.Block() as block:
            @block.sync
            def _(sp):
                def body(b, half, after, last):
                    u = HALF * b + half
                    for s in range(DEEP):
                        if s == DEEP - 3 and half == 1 and not last:
                            G.load(sp, after)
                        sp.wait_ge(stored[s], 16 * (u + 1))
                        sp.dma_start(x[:, s].rearrange("p h c -> p (h c)"), x1_dram[UNIT * u + s]).then_inc(loaded[s], 16)

                G.load(sp, 0)
                units(sp, body)

            @block.tensor
            def _(pe):
                G.start_tensor(pe)

                def body(b, half, after, last):
                    u = HALF * b + half
                    G.complete(pe, b, half)
                    for i in range(STEPS):
                        pe.wait_ge(added, STEPS * u + i + 1)
                        G.inverse_w(tabs, z[:, i % BANKS], half, BROWS * i).then_inc(spectral, 1)
                        if i in sums_at and not last:
                            G.tensor(pe, sums_at[i], after, 1 - half)

                units(pe, body)

            @block.vector
            def _(dve):
                dve.sem_inc(added, BANKS)
                G.start_vector(dve)

                def body(b, half, after, last):
                    u = HALF * b + half
                    for i in range(STEPS):
                        s, m = i // BANKS, i % BANKS
                        if m == 0:
                            dve.wait_ge(loaded[s], 16 * u + 16)
                        dve.wait_ge(spectral, STEPS * u + i + 1)
                        rows = x[:, s, BROWS * m:BROWS * (m + 1)].rearrange("p h c -> p (h c)")
                        nc.vector.tensor_tensor(rows, rows, z[:, m], ALU.add).then_inc(added, 1)
                        if i == 0 and not last:
                            G.prepare(dve, after, 1 - half)
                        if i in low_at and not last:
                            G.low(dve, *low_at[i], after, 1 - half)

                units(dve, body)

            @block.scalar
            def _(act):
                for s in range(DEEP):
                    act.sem_inc(stored[s], 16)
                G.start_scalar(act)

                def body(b, half, after, last):
                    u = HALF * b + half
                    for i in range(STEPS):
                        s, m = i // BANKS, i % BANKS
                        if i in high_at and not last:
                            G.high(act, *high_at[i], after, 1 - half)
                        if m == BANKS - 1:
                            act.wait_ge(added, STEPS * u + i + 1 + BANKS)
                            act.dma_start(out_dram[UNIT * u + s], x[:, s]).then_inc(stored[s], 16)

                units(act, body)
                for s in range(DEEP):
                    act.wait_ge(stored[s], 16 * (NU + 1))


def build(nc, d, out):
    def scratch(name, shape):
        return nc.dram_tensor(name, shape, F32, kind="Internal").ap()

    t0 = scratch("t0", [L0.KYR, B * H, C])
    t1 = scratch("t1", [L1.KYR, B * H, C])
    x0h, y0 = scratch("x0h", [2, RI, B, L0.M // 2, C]), scratch("y0", [RI, B, L0.M, C])
    x1h, y1 = scratch("x1h", [2, RI, B, L1.M // 2, C]), scratch("y1", [RI, B, L1.M, C])
    x1 = scratch("x1", [NCH, P, ROWS * JC])
    image = lambda a: a.rearrange("b (k h) (p j) c -> (b k) p h (j c)", k=CHUNKS, j=J)
    by_image = lambda a: a.rearrange("r b (x y) c -> r b x (y c)", x=KX)
    by_half = lambda a: a.rearrange("a r b (x y) c -> a r b x (y c)", x=KX // 2)
    by_octet = lambda a: a.rearrange("a r b (m q) c -> a (r b m) (q c)", m=8)
    by_round = lambda a: a.rearrange("r b (a n g m) c -> g n (r b) a (m c)", a=2, g=4, m=4)
    t_rows = lambda a: a.rearrange("k (n h) c -> n k (h c)", h=8)
    t_pairs = lambda a: a.rearrange("k (b p e) c -> b p k (e c)", p=P, e=PAIR)

    with Tiles(nc, "k") as t:
        k = {"ident": t.sb("ident", [P, P]), "fwd_h": t.sb("fwd_h", [P, HALF * 2 * 2 * KX]),
             "inv_h": t.sb("inv_h", [RI * KX, H]), "pairs": t.sb("pairs", [C, P]), "ones": t.sb("ones", [P, 8]),
             "wdiag": t.sb("wdiag", [P, P]), "wres": t.sb("wres", [C, C]), "bias": t.sb("bias", [B, C]),
             "wscaled": t.sb("wscaled", [P, B, P])}
        for n, lay in enumerate((L0, L1)):
            k[f"fwd_w{n}"] = t.sb(f"fwd_w{n}", [P, J * lay.KYR])
            if n:
                k[f"inv_w{n}h"] = t.sb(f"inv_w{n}h", [lay.K, J * P], F32R)
                k[f"inv_w{n}l"] = t.sb(f"inv_w{n}l", [lay.K, J * P], F32R)
        k["inv_w0"] = t.sb("inv_w0", [P, J * P], F32R)
        sq = t.sb("sq", [P, B * HALF, C])
        load_constants(nc, d, k)
        with Tiles(nc, "w0") as tw:
            wt = Weights0(nc, L0, tw, [d[n].rearrange("i o (a x) y r -> a i o (x y r)", a=Weights0.PARTS) for n in ("fw0", "fw1")])
            forward_w0(nc, L0, k, image(d["x"]), t_rows(t0), sq, wt)
            forward_h(nc, L0, "h0", k, t_pairs(t0), by_half(x0h))
            mix_modes(nc, L0, "m0", k, sq, by_octet(x0h), by_round(y0), wt)
        pixels0(nc, L0, k, image(d["x"]), by_image(y0), x1, t_rows(t1), sq)
        with Tiles(nc, "w1") as tw:
            wt = Weights1(nc, L1, tw, k, [d[n].rearrange("x y o i -> (x y) o i").rearrange("(a n q) o i -> a n o q i", a=2, q=4 * L1.RM)
                                          for n in ("kernel_re", "kernel_im")])
            forward_h(nc, L1, "h1", k, t_pairs(t1), by_half(x1h))
            mix_modes(nc, L1, "m1", k, sq, by_octet(x1h), by_round(y1), wt)
        pixels1(nc, L1, k, x1, by_image(y1), image(out))


def kernel(x, L0_conv_W_res, L0_conv_b_res, L0_conv_fw0, L0_conv_fw1, L1_conv_kernel_re, L1_conv_kernel_im):
    import concourse.bacc as bacc
    from concourse.bass_utils import run_bass_kernel_spmd

    nc = bacc.Bacc("TRN2", target_bir_lowering=False, num_devices=1)
    arrays = {"x": x, "W_res": L0_conv_W_res, "b_res": L0_conv_b_res, "fw0": L0_conv_fw0, "fw1": L0_conv_fw1,
              "kernel_re": L1_conv_kernel_re, "kernel_im": L1_conv_kernel_im}
    arrays = {n: np.ascontiguousarray(a) for n, a in arrays.items()} | tables()
    maps, d = {}, {}
    for n, a in arrays.items():
        maps[f"in_{n}"] = a
        d[n] = nc.dram_tensor(f"in_{n}", a.shape, mybir.dt.from_np(a.dtype), kind="ExternalInput").ap()
    out = nc.dram_tensor("out", (B, H, W, C), F32, kind="ExternalOutput").ap()
    build(nc, d, out)
    r = run_bass_kernel_spmd(nc, [maps], core_ids=[0])
    return r.results[0]["out"]
```

```python
from contextlib import ExitStack

import numpy as np

import concourse.bass as bass
from concourse import mybir

F32 = mybir.dt.float32
F32R = mybir.dt.float32r
ALU = mybir.AluOpType
ACT = mybir.ActivationFunctionType
AX = mybir.AxisListType

P = 128
B, H, W, C = 8, 256, 256, 64
J = W // P
JC = J * C
HALF = H // P
KX = 32
RI = 2
PIX = H * W
EPS = 1e-5

ROWS = 16
CHUNKS = H // ROWS
UNIT = CHUNKS // HALF
NCH = B * CHUNKS
PAIR = 2
BROWS = 4
BANKS = ROWS // BROWS
NB = BROWS * JC
SLOTS = 4
GC = 4


class Layer:

    def __init__(self, ky, groups):
        self.KY = ky
        self.KYR = 2 * ky
        self.NG = groups
        self.GP = P // groups
        self.LO = self.GP
        self.K = self.LO + self.KYR
        self.M = KX * ky
        self.NQ = self.M // 2 // 8
        self.RM = 4
        self.R = self.M // (2 * 4 * self.RM)
        self.RR = C // (groups * GC)
        self.pieces = [(a, min(a + 8, ky)) for a in range(0, ky, 8)] if ky % 8 == 0 else [(0, 6), (6, 12), (12, 17)]


L0 = Layer(16, 4)
L1 = Layer(17, 2)


def tables():
    out = {"ident": np.eye(P)}
    kx = np.concatenate([np.arange(16), np.arange(-16, 0)])
    h = np.arange(H)
    ph = 2 * np.pi * ((kx[None, :] * h[:, None]) % H) / H
    c, s = np.cos(ph), np.sin(ph)
    fh = np.stack([np.concatenate([c, -s], 1), np.concatenate([-s, -c], 1)], 1)
    out["fwd_h"] = fh.reshape(P, PAIR * 2 * 2 * KX)
    out["inv_h"] = np.concatenate([c, -s], 1).T
    w = (J * np.arange(P)[None, :] + np.arange(J)[:, None])
    for n, lay in enumerate((L0, L1)):
        ky = np.arange(lay.KY)
        pw = 2 * np.pi * ((ky[None, None] * w[..., None]) % W) / W
        f = np.concatenate([np.cos(pw), np.sin(pw)], -1)
        out[f"fwd_w{n}"] = f.transpose(1, 0, 2).reshape(P, -1)
        m = np.tile(np.where(ky == 0, 1.0, 2.0), 2) / PIX
        g = (f * m).transpose(2, 0, 1)
        k = np.zeros((lay.K, J, P))
        k[:lay.KYR] = g
        k[lay.LO:] = g
        out[f"inv_w{n}"] = (k if n else np.concatenate([k, k])).reshape(-1, J * P)
    pair = np.arange(P) // 2
    out["pairs"] = (pair[:C, None] == (np.arange(P) % C // 2)[None, :]).astype(float)
    out["ones"] = np.ones((P, 8))
    return {k: np.ascontiguousarray(v, np.float32) for k, v in out.items()}


class Tiles:

    def __init__(self, nc, tag):
        self.nc, self.tag, self.stack = nc, tag, ExitStack()

    def __enter__(self):
        return self

    def __exit__(self, *a):
        return self.stack.__exit__(*a)

    def sb(self, name, shape, dt=F32):
        return self.stack.enter_context(self.nc.sbuf_tensor(f"{self.tag}_{name}", shape, dt))

    def ps(self, name, shape):
        return self.stack.enter_context(self.nc.psum_tensor(f"{self.tag}_{name}", shape, F32))

    def sem(self, name):
        return self.stack.enter_context(self.nc.semaphore(f"{self.tag}_{name}"))

    def sems(self, name, n):
        return [self.sem(f"{name}{i}") for i in range(n)]


def settle(eng, sem):
    eng.sem_inc(sem, 1)


def load_rows(eng, dst, src, sem):
    for h in range(0, ROWS, ROWS // 2):
        eng.dma_start(dst[:, h:h + ROWS // 2], src[:, h:h + ROWS // 2]).then_inc(sem, 16)


LOADED = 32


class Chunks:

    def __init__(self, t, slots, dram, early):
        self.x = t.sb("x", [P, slots, ROWS, JC])
        self.loaded = t.sems("loaded", slots)
        self.slots, self.dram = slots, dram
        self.early = range(early)

    def load(self, eng, n, s):
        load_rows(eng, self.x[:, s], self.dram[n], self.loaded[s])


def load_constants(nc, d, k, chunks):
    with Tiles(nc, "c") as t:
        loaded, hi_done, written = t.sem("loaded"), t.sem("hi_done"), t.sem("written")
        raw = {0: t.sb("raw0", [P, J * P]), 1: t.sb("raw1", [L1.K, J * P])}
        hi0 = t.sb("hi0", [P, J * P], F32R)
        pairs = [(k["ident"], d["ident"]), (k["fwd_h"], d["fwd_h"]), (k["inv_h"], d["inv_h"]),
                 (k["fwd_w0"], d["fwd_w0"]), (k["fwd_w1"], d["fwd_w1"]), (k["pairs"], d["pairs"]),
                 (k["ones"], d["ones"]), (raw[0], d["inv_w0"]), (raw[1], d["inv_w1"])]
        with nc.Block() as block:
            @block.sync
            def _(sp):
                for dst, src in pairs:
                    sp.dma_start(dst[:], src).then_inc(loaded, 16)
                sp.wait_ge(hi_done, 1)
                for j in range(J):
                    sp.dma_start(k["wdiag"][j * C:(j + 1) * C, j * C:(j + 1) * C], d["W_res"]).then_inc(loaded, 16)
                sp.dma_start(k["wres"][:], d["W_res"]).then_inc(loaded, 16)
                sp.dma_start(k["bias"][:], d["b_res"].rearrange("(a c) -> a c", a=1).broadcast_to([B, C])).then_inc(loaded, 16)
                sp.wait_ge(loaded, 16 * (len(pairs) + J + 2))

            @block.scalar
            def _(act):
                for s in chunks.early:
                    chunks.load(act, s, s)

            @block.vector
            def _(dve):
                nc.vector.memset(k["wdiag"][:], 0.0).then_inc(hi_done, 1)
                dve.wait_ge(loaded, 16 * (len(pairs) + J + 2))
                nc.vector.tensor_copy(hi0[:], raw[0][:]).then_inc(hi_done, 1)
                nc.vector.tensor_copy(k["inv_w1h"][:], raw[1][:]).then_inc(hi_done, 1)
                dve.wait_ge(hi_done, 3)
                nc.vector.tensor_copy(k["inv_w0"][0:C], raw[0][0:C]).then_inc(written, 1)
                nc.vector.tensor_tensor(k["inv_w0"][C:P], raw[0][C:P], hi0[C:P].bitcast(F32), ALU.subtract).then_inc(written, 1)
                nc.vector.tensor_tensor(k["inv_w1l"][:], raw[1][:], k["inv_w1h"][:].bitcast(F32), ALU.subtract).then_inc(written, 1)


def forward_w0(nc, lay, k, chunks, t_dram, sq, wt):
    with Tiles(nc, "a") as t:
        x, loaded = chunks.x, chunks.loaded
        q = t.sb("q", [P, 2, ROWS, JC])
        part = t.sb("part", [P, UNIT, C])
        ts = t.sb("ts", [P, 2, 512])
        tp = t.ps("tp", [P, 2, 512])
        stored = t.sems("stored", 2)
        names = ("summed", "copied", "squared", "reduced", "final", "tick")
        summed, copied, squared, reduced, final, tick = (t.sem(n) for n in names)
        PAIRS = SLOTS // 2
        N = NCH // SLOTS
        with nc.Block() as block:
            @block.sync
            def _(sp):
                with sp.Fori(1, N) as i:
                    for s in range(SLOTS):
                        if s % 2 == 0:
                            sp.wait_ge(summed, PAIRS * i + s // 2 + 1)
                            settle(sp, tick)
                            sp.wait_ge(squared, SLOTS * i + s + 2)
                        chunks.load(sp, SLOTS * i + s, s)

            @block.tensor
            def _(pe):
                pe.sem_inc(summed, PAIRS)
                with pe.Fori(0, N) as i:
                    for r in range(PAIRS):
                        for s in (2 * r, 2 * r + 1):
                            pe.wait_ge(loaded[s], LOADED * (i + 1))
                        pe.wait_ge(copied, PAIRS * i + r + 1)
                        for j in range(J):
                            for g in range(4):
                                s, h = 2 * r + g // 2, 8 * (g % 2)
                                mm = nc.tensor.matmul(tp[32 * g:32 * g + lay.KYR, r], k["fwd_w0"][:, j * lay.KYR:(j + 1) * lay.KYR],
                                                      x[:, s, h:h + 8, j * C:(j + 1) * C], start=(j == 0), stop=(j == J - 1))
                        mm.then_inc(summed, 1)

            @block.scalar
            def _(act):
                act.sem_inc(copied, PAIRS)
                act.sem_inc(squared, SLOTS)
                for r in range(PAIRS):
                    act.sem_inc(stored[r], 64)
                wt.load(act, 0)

                def store_t(i, r):
                    act.wait_ge(summed, PAIRS * i + r + 1 + PAIRS)
                    act.wait_ge(stored[r], 64 * (i + 1))
                    nc.scalar.activation(ts[:, r], tp[:, r], ACT.Copy).then_inc(copied, 1)
                    act.wait_ge(copied, PAIRS * i + r + 1 + PAIRS)
                    for g in range(4):
                        act.dma_start(t_dram[4 * (PAIRS * i + r) + g], ts[32 * g:32 * g + lay.KYR, r]).then_inc(stored[r], 16)

                def body(i, first):
                    for s in range(SLOTS):
                        act.wait_ge(loaded[s], LOADED * (i + 1))
                        act.wait_ge(reduced, SLOTS * i + s + 1)
                        nc.scalar.activation(q[:, s % 2], x[:, s], ACT.Square).then_inc(squared, 1)
                        if s == 2:
                            store_t(i, 0)
                        if s == 0 and not first:
                            store_t(i - 1, 1)

                body(0, True)
                with act.Fori(1, N) as i:
                    body(i, False)
                store_t(N - 1, 1)
                for r in range(PAIRS):
                    act.wait_ge(stored[r], 64 * (N + 1))

            @block.vector
            def _(dve):
                dve.sem_inc(reduced, 2)
                dve.sem_inc(final, 1)
                with dve.Fori(0, B * HALF) as u:
                    for s in range(UNIT):
                        dve.wait_ge(squared, UNIT * u + s + 1 + SLOTS)
                        if s == 0:
                            dve.wait_ge(final, u + 1)
                        nc.vector.tensor_reduce(part[:, s], q[:, s % 2].rearrange("p h (j c) -> p c h j", j=J),
                                                AX.XY, ALU.add).then_inc(reduced, 1)
                    dve.wait_ge(reduced, UNIT * (u + 1) + 2)
                    nc.vector.tensor_reduce(sq[:, u], part[:].rearrange("p n c -> p c n"), AX.X, ALU.add).then_inc(final, 1)


def forward_h(nc, lay, tag, k, t_dram, xh_dram):
    with Tiles(nc, tag) as t:
        u = t.sb("u", [P, 2, lay.KYR, PAIR, C])
        xs = t.sb("xs", [P, 2, lay.KY * C])
        NP = len(lay.pieces)
        ps = t.ps("ps", [P, 2, NP, 512])
        loaded, stored = t.sems("loaded", 2), t.sems("stored", 2)
        summed, copied = t.sem("summed"), t.sem("copied")
        PARTS = 4
        cuts = [lay.KYR * n // PARTS for n in range(PARTS + 1)]
        place = [slice(2 * KX * (n % 2), 2 * KX * (n % 2 + 1)) for n in range(NP)]
        with nc.Block() as block:
            @block.sync
            def _(sp):
                with sp.Fori(0, B // 2) as i:
                    for s in range(2):
                        sp.wait_ge(summed, 2 * i + s + 1)
                        for a, e in zip(cuts, cuts[1:]):
                            sp.dma_start(u[:, s, a:e].rearrange("p k e c -> p k (e c)"), t_dram[2 * i + s][:, a:e]).then_inc(loaded[s], 16)

            @block.tensor
            def _(pe):
                pe.sem_inc(summed, 2)
                with pe.Fori(0, B // 2) as i:
                    for s in range(2):
                        pe.wait_ge(loaded[s], 16 * PARTS * (i + 1))
                        pe.wait_ge(copied, 2 * i + s + 1)
                        for first in range(0, NP, 2):
                            for e in range(PAIR):
                                for cs in range(2):
                                    tab = k["fwd_h"][:, (e * 2 + cs) * 2 * KX:(e * 2 + cs + 1) * 2 * KX]
                                    for n in range(first, min(first + 2, NP)):
                                        a, b = lay.pieces[n]
                                        mm = nc.tensor.matmul(ps[place[n], s, n, 0:(b - a) * C], tab,
                                                              u[:, s, cs * lay.KY + a:cs * lay.KY + b, e],
                                                              start=(e == 0 and cs == 0), stop=(e == PAIR - 1 and cs == 1))
                        mm.then_inc(summed, 1)

            @block.scalar
            def _(act):
                act.sem_inc(copied, 2)
                for s in range(2):
                    act.sem_inc(stored[s], 16 * 2 * NP)
                with act.Fori(0, B // 2) as i:
                    for s in range(2):
                        act.wait_ge(summed, 2 * i + s + 1 + 2)
                        act.wait_ge(stored[s], 16 * 2 * NP * (i + 1))
                        for n, (a, e) in enumerate(lay.pieces):
                            last = nc.scalar.activation(xs[place[n], s, a * C:e * C], ps[place[n], s, n, 0:(e - a) * C], ACT.Copy)
                        last.then_inc(copied, 1)
                        act.wait_ge(copied, 2 * i + s + 1 + 2)
                        for n, (a, e) in enumerate(lay.pieces):
                            for ri in range(RI):
                                row = place[n].start + ri * KX
                                act.dma_start(xh_dram[:, ri, 2 * i + s, :, a * C:e * C],
                                              xs[row:row + KX, s, a * C:e * C]).then_inc(stored[s], 16)
                for s in range(2):
                    act.wait_ge(stored[s], 16 * 2 * NP * (B // 2 + 1))


def mix_modes(nc, lay, tag, k, sq, xh_dram, y_dram, wt, chunks=None):
    M, NQ, R, RM = lay.M, lay.NQ, lay.R, lay.RM
    Q2 = 2
    NT = NQ // Q2
    UR = wt.UNROLL
    LOOP = (R - 1) // UR
    YS = 4
    with Tiles(nc, tag) as t:
        xl = t.sb("xl", [P, 2, NQ * C])
        xt = t.sb("xt", [P, M // 2, RI, B])
        xr = t.sb("xr", [P, 2, 4, RM, 3, B])
        ys = t.sb("ys", [P, YS, 2, RM * C])
        st = t.sb("st", [P, 10, B])
        bt = t.sb("bt", [B, C])
        pt = t.ps("pt", [P, 2, 512])
        py = t.ps("py", [P, 2, 2, 512])
        names = ("xl", "statistic_mm", "statistic", "turned", "scaled", "dc", "staged", "mixed", "copied", "zeroed", "ready", "tick")
        S = {n: t.sem(n) for n in names}
        stored = t.sems("stored", YS)
        wt.begin(t, S)
        DC, SSQ, MEAN, EX2, MSQ, VAR, SD, SCALE, SHIFT, SHIFT_DC = range(10)
        with nc.Block() as block:
            @block.sync
            def _(sp):
                def store(r, z):
                    sp.wait_ge(S["ready"], r + 2)
                    for g in range(4):
                        sp.dma_start(y_dram[g][r], ys[32 * g:32 * g + RI * B, z]).then_inc(stored[z], 16)

                for half in range(2):
                    sp.dma_start(xl[:, half], xh_dram[half]).then_inc(S["xl"], 16)
                wt.prefetch(sp)
                U = wt.UNROLL
                with sp.Fori(1, R // U) as i:
                    for z in range(U):
                        wt.reload(sp, U * i + z, z)
                        store(U * (i - 1) + z, z % YS)
                for r in range(R // U * U, R):
                    wt.reload(sp, r, r % U)
                for r in range((R // U - 1) * U, R):
                    store(r, r % YS)
                    if chunks and r - (R - 1) + len(chunks.early) in chunks.early:
                        s = r - (R - 1) + len(chunks.early)
                        chunks.load(sp, s, s)
                for z in range(YS):
                    sp.wait_ge(stored[z], 16 * 4 * len(range(z, R, YS)))

            @block.tensor
            def _(pe):
                pe.sem_inc(S["mixed"], 2)
                pe.wait_ge(S["xl"], 32)

                def turn(q):
                    for half in range(2):
                        tr = nc.tensor.matmul(pt[half * C:(half + 1) * C, (q // Q2) % 2, (q % Q2) * P:(q % Q2 + 1) * P],
                                              xl[:, half, q * C:(q + 1) * C], k["ident"][:], start=True, stop=True,
                                              skip_group_check=True)
                    return tr

                def mix_round(r, z):
                    wt.tensor(pe, r)
                    pe.wait_ge(S["staged"], r + 1)
                    pe.wait_ge(S["copied"], r + 1)
                    settle(pe, S["tick"])
                    for m in range(RM):
                        for part in range(2):
                            for g in range(4):
                                for half in range(2):
                                    rows = slice(half * C, half * C + C)
                                    out = py[32 * g:32 * g + RI * B, z, half, m * C:(m + 1) * C]
                                    lhs = xr[rows, z, g, m, 1 - part:3 - part]
                                    mm = nc.tensor.matmul(out, lhs, wt.rhs(half, g, m, part, z), start=(part == 0),
                                                          stop=(part == 1), skip_group_check=True)
                    mm.then_inc(S["mixed"], 1)

                pe.wait_ge(S["zeroed"], 1)
                for b in range(B):
                    for half in range(HALF):
                        nc.tensor.matmul(py[0:C, 0, 0, b:b + 1], sq[:, HALF * b + half], k["ones"][:, 0:1], start=(half == 0),
                                         stop=(half == HALF - 1), skip_group_check=True)
                for q in range(Q2):
                    turn(q).then_inc(S["turned"], 1)
                pe.wait_ge(S["statistic"], 2)
                nc.tensor.matmul(py[:, 1, 0, 0:2 * B], k["pairs"][:], st[0:C, DC:SSQ + 1], start=True, stop=True,
                                 skip_group_check=True).then_inc(S["statistic_mm"], 1)
                if lay is L0:
                    pe.wait_ge(S["statistic"], 9)
                    nc.tensor.matmul(py[0:B, 1, 0, 128:128 + C], st[0:C, SHIFT], k["wres"][:], start=True, stop=True,
                                     skip_group_check=True).then_inc(S["statistic_mm"], 1)
                for n in range(1, NT):
                    if n >= 2:
                        pe.wait_ge(S["scaled"], n - 1)
                    for q in range(Q2 * n, Q2 * n + Q2):
                        turn(q).then_inc(S["turned"], 1)
                wt.tensor_start(pe)
                with pe.Fori(0, LOOP) as i:
                    for z in range(UR):
                        wt.tensor_next(pe, UR * i + z + 1, (z + 1) % UR, i + (z + 1) // UR)
                        mix_round(UR * i + z, z % 2)
                for r in range(UR * LOOP, R):
                    if r + 1 < R:
                        wt.tensor_next(pe, r + 1, (r + 1) % UR, (r + 1) // UR)
                    mix_round(r, r % 2)

            @block.scalar
            def _(act):
                act.wait_ge(S["statistic"], 6)
                nc.scalar.activation(st[:, SD], st[:, VAR], ACT.Sqrt).then_inc(S["statistic"], 1)
                wt.scalar(act)

            @block.vector
            def _(dve):
                nc.vector.memset(py[:], 0.0).then_inc(S["zeroed"], 1)
                dve.sem_inc(S["ready"], 1)
                dve.sem_inc(S["copied"], 2)
                dve.wait_ge(S["turned"], Q2)
                first = pt[:, 0, 0:P].rearrange("p (r b m) -> p r b m", r=RI, b=B)
                nc.vector.tensor_copy(st[0:C, DC], first[0:C, 0, :, 0]).then_inc(S["statistic"], 1)
                nc.vector.tensor_copy(st[0:C, SSQ], py[0:C, 0, 0, 0:B]).then_inc(S["statistic"], 1)
                dve.wait_ge(S["statistic_mm"], 1)
                n = 1.0 / (2 * PIX)
                nc.vector.tensor_scalar(st[:, MEAN], py[:, 1, 0, 0:B], n, None, ALU.mult).then_inc(S["statistic"], 1)
                nc.vector.tensor_scalar(st[:, EX2], py[:, 1, 0, B:2 * B], n, EPS, ALU.mult, ALU.add).then_inc(S["statistic"], 1)
                dve.wait_ge(S["statistic"], 4)
                nc.vector.tensor_tensor(st[:, MSQ], st[:, MEAN], st[:, MEAN], ALU.mult).then_inc(S["statistic"], 1)
                dve.wait_ge(S["statistic"], 5)
                nc.vector.tensor_tensor(st[:, VAR], st[:, EX2], st[:, MSQ], ALU.subtract).then_inc(S["statistic"], 1)
                dve.wait_ge(S["statistic"], 7)
                nc.vector.reciprocal(st[:, SCALE], st[:, SD]).then_inc(S["statistic"], 1)
                dve.wait_ge(S["statistic"], 8)
                nc.vector.tensor_tensor(st[:, SHIFT], st[:, SCALE], st[:, MEAN], ALU.mult).then_inc(S["statistic"], 1)
                dve.wait_ge(S["statistic"], 9)
                nc.vector.tensor_scalar(st[:, SHIFT_DC], st[:, SHIFT], float(PIX), None, ALU.mult).then_inc(S["statistic"], 1)

                scale = st[:, SCALE].rearrange("p (a b) -> p a b", a=1).broadcast_to([P, 8, B])
                by_q = xt[:].rearrange("p (m q) r b -> p q r m b", m=8)
                for n in range(NT):
                    dve.wait_ge(S["turned"], Q2 * (n + 1))
                    for q in range(Q2):
                        for ri in range(RI):
                            src = pt[:, n % 2, q * P:(q + 1) * P].rearrange("p (r b m) -> p r m b", r=RI, b=B)[:, ri]
                            last = nc.vector.tensor_tensor(by_q[:, Q2 * n + q, ri], src, scale, ALU.mult)
                    last.then_inc(S["scaled"], 1)
                dve.wait_ge(S["scaled"], NT)
                dve.wait_ge(S["statistic"], 10)
                nc.vector.tensor_tensor(xt[0:C, 0, 0], xt[0:C, 0, 0], st[0:C, SHIFT_DC], ALU.subtract).then_inc(S["dc"], 1)
                if lay is L0:
                    dve.wait_ge(S["statistic_mm"], 2)
                    nc.vector.tensor_tensor(bt[:], k["bias"][:], py[0:B, 1, 0, 128:128 + C], ALU.subtract).then_inc(S["dc"], 1)
                    for b in range(B):
                        nc.vector.tensor_scalar(k["wscaled"][:, b], k["wdiag"][:], st[:, SCALE, b:b + 1], None,
                                                ALU.mult).then_inc(S["dc"], 1)
                    dve.wait_ge(S["dc"], B + 2)
                else:
                    dve.wait_ge(S["dc"], 1)
                by_round = xt[:].rearrange("p (r g m) s b -> p r g m (s b)", g=4, r=R)

                def stage(r, z):
                    for m in range(RM):
                        nc.vector.tensor_copy(xr[:, z, :, m, 1:3].rearrange("p g s b -> p g (s b)"), by_round[:, r, :, m])
                        last = nc.vector.tensor_scalar(xr[:, z, :, m, 0], by_round[:, r, :, m, B:2 * B], -1.0, None, ALU.mult)
                    last.then_inc(S["staged"], 1)

                def copy_out(r, z, y, n):
                    dve.wait_ge(S["mixed"], r + 3)
                    if not (isinstance(n, int) and n == 0):
                        dve.wait_ge(stored[y], 16 * 4 * n)
                    cp = nc.vector.tensor_copy(ys[:, y], py[:, z, :, 0:RM * C])
                    cp.then_inc(S["copied"], 1)
                    if lay is L0 and isinstance(r, int) and r == 0:
                        dve.wait_ge(S["copied"], 3)
                        cp = nc.vector.scalar_tensor_tensor(out=ys[0:B, 0, 0, 0:C], in0=bt[:], scalar=float(PIX),
                                                            in1=ys[0:B, 0, 0, 0:C], op0=ALU.mult, op1=ALU.add)
                        cp.then_inc(S["ready"], 1)
                    else:
                        dve.wait_ge(S["copied"], r + 3)
                        dve.sem_inc(S["ready"], 1)

                def round_(r, z, y, n):
                    if not (isinstance(r, int) and r + 1 >= R):
                        dve.wait_ge(S["mixed"], r + 2)
                        stage(r + 1, 1 - z)
                    copy_out(r, z, y, n)

                stage(0, 0)
                for r in range(YS):
                    round_(r, r % 2, r, 0)
                FULL = (R - 1) // YS
                with dve.Fori(1, FULL) as i:
                    for y in range(YS):
                        round_(YS * i + y, y % 2, y, i)
                for r in range(YS * FULL, R):
                    round_(r, r % 2, r % YS, r // YS)


class Weights0:
    UNROLL = 4
    PARTS = 4
    LOADS = 4

    def __init__(self, nc, lay, t, weights_dram):
        self.nc, self.lay, self.dram = nc, lay, weights_dram
        self.raw = t.sb("raw", [P, self.PARTS, C, lay.M // 2 * RI // self.PARTS])
        self.loaded = t.sems("loaded", self.PARTS)

    def load(self, eng, part):
        for half in range(2):
            for o in range(0, C, 2 * C // self.LOADS):
                cols = slice(o, o + 2 * C // self.LOADS)
                eng.dma_start(self.raw[half * C:(half + 1) * C, part, cols],
                              self.dram[half][part][:, cols]).then_inc(self.loaded[part], 16)

    def prefetch(self, sp):
        for part in range(1, self.PARTS):
            self.load(sp, part)

    def begin(self, t, S):
        self.S = S
        self.w = t.sb("w", [P, 2, 4 * self.lay.RM, RI * C])
        self.packed = t.sem("w_packed")

    def reload(self, sp, r, slot):
        pass

    def tensor_start(self, pe):
        pass

    def tensor_next(self, pe, r, slot, n):
        pass

    def tensor(self, pe, r):
        pe.wait_ge(self.packed, r + 1)

    def scalar(self, act):
        rounds = self.lay.R // self.PARTS
        for part in range(self.PARTS):
            act.wait_ge(self.loaded[part], 16 * self.LOADS)
            by_round = self.raw[:, part].rearrange("p o (r x) -> p r x o", r=rounds)
            with act.Fori(0, rounds // 2) as i:
                for z in range(2):
                    act.wait_ge(self.S["mixed"], rounds * part + 2 * i + z + 1)
                    dst = self.w[:, z].rearrange("p q (i o) -> p (q i) o", i=RI)
                    self.nc.scalar.activation(dst, by_round[:, 2 * i + z], ACT.Copy).then_inc(self.packed, 1)

    def rhs(self, half, g, m, part, z):
        return self.w[half * C:half * C + C, z, g * self.lay.RM + m, part * C:part * C + C]


class Weights1:
    UNROLL = 4

    def __init__(self, nc, lay, t, k, weights_dram):
        self.nc, self.lay, self.k, self.dram = nc, lay, k, weights_dram
        self.raw = t.sb("raw", [P, self.UNROLL, 4 * lay.RM, 2, C])
        self.loaded = t.sems("loaded", self.UNROLL)

    def load(self, eng, r, slot):
        for ri in range(RI):
            for half in range(2):
                eng.dma_start(self.raw[ri * C:(ri + 1) * C, slot, :, half], self.dram[ri][half][r]).then_inc(self.loaded[slot], 16)

    def prefetch(self, sp):
        for r in range(self.UNROLL):
            self.load(sp, r, r)

    def begin(self, t, S):
        self.S = S
        self.w = t.sb("w", [P, 2, 4 * self.lay.RM, P])
        self.ps = t.ps("pw", [P, 2, 512])
        self.turned, self.copied = t.sem("w_turned"), t.sem("w_copied")

    def reload(self, sp, r, slot):
        sp.wait_ge(self.turned, 4 * (r - self.UNROLL) + 8)
        self.load(sp, r, slot)

    def tensor_start(self, pe):
        pe.sem_inc(self.turned, 4)
        self.tensor_next(pe, 0, 0, 0)

    def tensor_next(self, pe, r, slot, n):
        pe.wait_ge(self.loaded[slot], 64 * (n + 1))
        for b in range(4):
            pe.wait_ge(self.copied, 4 * r + b + 1)
            for q in range(4 * b, 4 * b + 4):
                mm = self.nc.tensor.transpose(self.ps[:, b % 2, (q % 4) * P:(q % 4 + 1) * P],
                                              self.raw[:, slot, q].rearrange("p a c -> p (a c)"), self.k["ident"][:])
            mm.then_inc(self.turned, 1)

    def tensor(self, pe, r):
        pe.wait_ge(self.copied, 4 * r + 6)

    def scalar(self, act):
        act.sem_inc(self.copied, 2)

        def body(r, z):
            act.wait_ge(self.S["mixed"], r + 1)
            for b in range(4):
                act.wait_ge(self.turned, 4 * r + b + 5)
                self.nc.scalar.activation(self.w[:, z, 4 * b:4 * b + 4].rearrange("p q c -> p (q c)"), self.ps[:, b % 2],
                                          ACT.Copy).then_inc(self.copied, 1)
        with act.Fori(0, self.lay.R // 2) as i:
            for z in range(2):
                body(2 * i + z, z)
        body(self.lay.R - 1, 0)

    def rhs(self, half, g, m, part, z):
        return self.w[half * C:half * C + C, z, g * self.lay.RM + m, part * C:part * C + C]


class InverseH:

    def __init__(self, nc, lay, t, k, y_dram, spare, banks):
        self.nc, self.lay, self.k, self.y_dram = nc, lay, k, y_dram
        self.raw = t.sb("y_raw", [RI * KX, lay.KY, C])
        self.y = t.sb("y", [RI * KX, C, lay.GP])
        self.g = t.sb("g", [P, 2, P, C], F32R)
        self.banks = banks
        self.ps = t.ps("pg", [P, banks, 512])
        self.ahead = lay.NG * (banks - 1)
        self.first = spare + [self.ps[:, n] for n in range(banks)]
        self.loaded, self.ready = t.sem("y_loaded"), t.sem("y_ready")
        self.summed, self.hi, self.lo = (t.sem("g_" + n) for n in ("summed", "hi", "lo"))
        self.doubled = t.sems("g_doubled", 2)
        self.tick = t.sem("g_tick")

    def load(self, sp, b):
        sp.wait_ge(self.ready, self.TURNS * b + 1)
        for ri in range(RI):
            sp.dma_start(self.raw[ri * KX:(ri + 1) * KX].rearrange("p k c -> p (k c)"), self.y_dram[ri][b]).then_inc(self.loaded, 16)

    def start_tensor(self, pe):
        pe.sem_inc(self.summed, 1)
        for r in range(self.lay.RR):
            self.tensor(pe, r, 0, 0, True)

    def start_scalar(self, act):
        for r in range(self.lay.RR):
            for g in range(self.lay.NG):
                self.high(act, r, g, 0, 0, True)

    def start_vector(self, dve):
        dve.sem_inc(self.lo, self.ahead + 1)
        if self.lay.GP > self.lay.KYR:
            self.nc.vector.memset(self.y[:, :, self.lay.KYR:], 0.0).then_inc(self.ready, 1)
        else:
            dve.sem_inc(self.ready, 1)
        for n in range(self.TURNS):
            self.turn(dve, 0, n)
        for r in range(self.lay.RR):
            for g in range(self.lay.NG):
                self.low(dve, r, g, 0, 0, True)

    def rounds(self, b, half):
        return self.lay.RR * (HALF * b + half)

    TURNS = 3

    def turn(self, dve, b, n):
        if n == 0:
            dve.wait_ge(self.summed, self.rounds(b, 0) + 1)
            dve.wait_ge(self.loaded, 16 * RI * (b + 1))
        KY = self.lay.KY
        raw = self.raw[:].rearrange("p k c -> p c k")
        if n == 0:
            step = self.nc.vector.tensor_copy(self.y[:, :, 0:KY], raw)
        elif n == 1:
            step = self.nc.vector.tensor_copy(self.y[KX:, :, KY:2 * KY], raw[0:KX])
        else:
            step = self.nc.vector.tensor_scalar(self.y[0:KX, :, KY:2 * KY], raw[KX:], -1.0, None, ALU.mult)
        step.then_inc(self.ready, 1)

    def bank(self, r, first):
        return self.first[r % len(self.first)] if first else self.ps[:, r % self.banks]

    def tensor(self, pe, r, b, half, first=False):
        lay = self.lay
        pe.wait_ge(self.ready, self.TURNS * (b + 1) + 1)
        if not first:
            pe.wait_ge(self.lo, lay.NG * (self.rounds(b, half) + r) + 1)
        settle(pe, self.tick)
        for cc in range(GC):
            for g in range(lay.NG):
                c = (g * lay.RR + r) * GC + cc
                mm = self.nc.tensor.matmul(self.bank(r, first)[lay.GP * g:lay.GP * (g + 1), cc * P:(cc + 1) * P],
                                           self.y[:, c], self.k["inv_h"][:, half * P:(half + 1) * P],
                                           start=True, stop=True, skip_group_check=True)
        mm.then_inc(self.summed, 1)

    def piece(self, r, g, first, count):
        lay = self.lay
        c = (g * lay.RR + r) * GC
        rows = self.bank(r, first)[lay.GP * g:lay.GP * g + count]
        return rows.rearrange("p (c h) -> p h c", h=P), slice(c, c + GC)

    def high(self, act, r, g, b, half, first=False):
        lay = self.lay
        if g == 0:
            act.wait_ge(self.summed, self.rounds(b, half) + r + 2)
        src, cols = self.piece(r, g, first, lay.GP)
        self.nc.scalar.activation(self.g[0:lay.GP, half, :, cols], src, ACT.Copy).then_inc(self.hi, 1)

    def low(self, dve, r, g, b, half, first=False):
        lay = self.lay
        dve.wait_ge(self.hi, lay.NG * (self.rounds(b, half) + r) + g + 1)
        src, cols = self.piece(r, g, first, lay.KYR)
        self.nc.vector.tensor_tensor(self.g[lay.LO:lay.LO + lay.KYR, half, :, cols], src,
                                     self.g[0:lay.KYR, half, :, cols].bitcast(F32), ALU.subtract).then_inc(self.lo, 1)

    def complete(self, eng, b, half):
        eng.wait_ge(self.lo, self.lay.NG * (self.rounds(b, half) + self.lay.RR) + self.ahead + 1)

    def double(self, sp, b, half):
        self.complete(sp, b, half)
        rows = 2 * self.lay.LO
        sp.dma_start(self.g[rows:2 * rows, half].rearrange("p h c -> p (h c)").bitcast(F32),
                     self.g[0:rows, half].rearrange("p h c -> p (h c)").bitcast(F32)).then_inc(self.doubled[half], 16)

    def inverse_w1(self, tab, z, slot, row):
        out = z.rearrange("p (h j c) -> p j h c", j=J, c=C)
        for j in range(J):
            mm = self.nc.tensor.matmul(out[:, j], tab[:, j * P:(j + 1) * P], self.g[:, slot, row:row + BROWS],
                                       start=(j == 0), stop=True, skip_group_check=True)
        return mm

    def inverse_w(self, tables, z, slot, row):
        lay = self.lay
        out = z.rearrange("p (h j c) -> p j h c", j=J, c=C)
        for n, tab in enumerate(tables):
            for j in range(J):
                mm = self.nc.tensor.matmul(out[:, j], tab[:, j * P:(j + 1) * P], self.g[0:lay.K, slot, row:row + BROWS],
                                           start=(n == 0 and j == 0), stop=(n == 1), skip_group_check=True)
        return mm


def is_first(b):
    return isinstance(b, int) and b == 0


def units(eng, body):
    body(0, 0, 0, 1)
    with eng.Fori(0, B - 2) as i:
        body(i, 1, i + 1, None)
        body(i + 1, 0, i + 1, i + 2)
    body(B - 2, 1, B - 1, None)
    body(B - 1, 0, B - 1, None)
    body(B - 1, 1, None, None)


def pixels0(nc, lay, k, x_dram, y_dram, x1_dram, t_dram, sq):
    NU = B * HALF
    STEPS = UNIT * BANKS
    HR = ROWS // 2
    with Tiles(nc, "b") as t:
        x = t.sb("x", [P, SLOTS, ROWS, JC])
        x1 = t.sb("x1", [P, SLOTS, ROWS, JC])
        xt = t.sb("xt", [P, 2, NB])
        q = t.sb("q", [P, 2, HR, JC])
        part = t.sb("part", [P, 2 * UNIT, C])
        ts = t.sb("ts", [P, 2, 512])
        pt = t.ps("pt", [P, 2, NB])
        z = t.ps("z", [P, BANKS, NB])
        tp = t.ps("tp", [P, 512])
        G = InverseH(nc, lay, t, k, y_dram, [z[:, m] for m in range(BANKS)], 1)
        loaded, x1_stored, t_stored = t.sems("loaded", SLOTS), t.sems("x1_stored", SLOTS), t.sems("t_stored", 2)
        names = ("turned", "turned_copied", "pixels", "silu", "added", "summed", "t_copied", "squared", "reduced", "final")
        turned, turned_copied, pixels, silu, added, summed, t_copied, squared, reduced, final = (t.sem(n) for n in names)
        APART = lay.NG + 2
        sums_at = {APART * r: r for r in range(lay.RR)}
        high_at = {APART * r + 1 + g: (r, g) for r in range(lay.RR) for g in range(lay.NG)}
        low_at = {APART * r + 4 + g: (r, g) for r in range(lay.RR) for g in range(lay.NG)}
        AFTER = {"forward": 6, "square0": 4, "square1": 6, "t_copy": 7, "reduce0": 7, "reduce1": 9, "total": 10}
        DOUBLE_AT = UNIT - 1
        assert max(low_at) < BANKS * DOUBLE_AT

        def due(kinds, step, first=False):
            for kind in kinds:
                s, rest = divmod(step - AFTER[kind], BANKS)
                if rest == 0 and s < UNIT and not (first and s < 0):
                    yield kind, s

        TURN_AT = {STEPS - G.TURNS + n: n for n in range(G.TURNS)}
        TAIL = range(STEPS, STEPS + 2 * BANKS + 3)

        with nc.Block() as block:
            @block.sync
            def _(sp):
                for s in range(SLOTS):
                    sp.sem_inc(x1_stored[s], 16)
                for s in range(2):
                    sp.sem_inc(t_stored[s], 32)

                def x1_store(n, s):
                    sp.wait_ge(added, 2 * (n + 1))
                    sp.dma_start(x1_dram[n], x1[:, s % SLOTS].rearrange("p h c -> p (h c)")).then_inc(x1_stored[s % SLOTS], 16)

                def t_store(n, s):
                    sp.wait_ge(t_copied, n + 2)
                    for g in range(2):
                        sp.dma_start(t_dram[2 * n + g], ts[C * g:C * g + L1.KYR, s % 2]).then_inc(t_stored[s % 2], 16)

                def body(b, half, after, new):
                    u, first, last = HALF * b + half, is_first(b), after is None
                    for s in range(UNIT):
                        n = UNIT * u + s
                        if s == 1 and new is not None:
                            G.load(sp, new)
                        if s == DOUBLE_AT and not last:
                            G.double(sp, after, 1 - half)
                        if not (first and s == 0):
                            sp.wait_ge(added, 2 * n)
                        if not (last and s + 3 >= UNIT):
                            load_rows(sp, x[:, (s + 3) % SLOTS], x_dram[n + 3], loaded[(s + 3) % SLOTS])
                        if not (first and s < 1):
                            x1_store(n - 1, s + SLOTS - 1)
                        if not (first and s < 2):
                            t_store(n - 2, s)

                G.load(sp, 0)
                for s in range(SLOTS - 1):
                    load_rows(sp, x[:, s], x_dram[s], loaded[s])
                G.double(sp, 0, 0)
                units(sp, body)
                x1_store(NCH - 1, SLOTS - 1)
                t_store(NCH - 2, 0)
                t_store(NCH - 1, 1)
                for s in range(SLOTS):
                    sp.wait_ge(x1_stored[s], 16 * (NCH // SLOTS + 1))
                for s in range(2):
                    sp.wait_ge(t_stored[s], 32 * (NCH // 2 + 1))

            @block.tensor
            def _(pe):
                pe.sem_inc(summed, SLOTS)
                G.start_tensor(pe)

                def turn(u, i):
                    s, m = i // BANKS, i % BANKS
                    if m == 0:
                        pe.wait_ge(loaded[s % SLOTS], LOADED * (2 * u + s // SLOTS + 1))
                    for h in range(BROWS):
                        tr = nc.tensor.transpose(pt[:, m % 2, h * P:(h + 1) * P], x[:, s % SLOTS, BROWS * m + h], k["ident"][:])
                    tr.then_inc(turned, 1)

                def forward(u, s):
                    n = UNIT * u + s
                    pe.wait_ge(added, 2 * n + 2)
                    pe.wait_ge(t_copied, n + 1)
                    for j in range(J):
                        for g in range(2):
                            mm = nc.tensor.matmul(tp[C * g:C * g + L1.KYR], k["fwd_w1"][:, j * L1.KYR:(j + 1) * L1.KYR],
                                                  x1[:, s % SLOTS, 8 * g:8 * g + 8, j * C:(j + 1) * C], start=(j == 0), stop=(j == J - 1))
                    mm.then_inc(summed, 1)

                def body(b, half, after, new):
                    u, first, last = HALF * b + half, is_first(b), after is None
                    pe.wait_ge(G.doubled[half], 16 * (b + 1))
                    for i in range(STEPS):
                        s, m = i // BANKS, i % BANKS
                        bank = STEPS * u + i
                        if not (last and i + 1 == STEPS):
                            turn(u + (i + 1) // STEPS, (i + 1) % STEPS)
                        pe.wait_ge(silu, bank + 1)
                        G.inverse_w1(k["inv_w0"], z[:, m], half, ROWS * s + BROWS * m)
                        pe.wait_ge(turned_copied, bank + 1)
                        for h in range(BROWS):
                            cols = slice(h * P, (h + 1) * P)
                            mm = nc.tensor.matmul(z[:, m, cols], xt[:, m % 2, cols], k["wscaled"][:, b],
                                                  start=False, stop=True, skip_group_check=True)
                        mm.then_inc(pixels, 1)
                        for _, c in due(["forward"], i, first):
                            forward(u, c)
                        if i in sums_at and not last:
                            G.tensor(pe, sums_at[i], after, 1 - half)

                turn(0, 0)
                units(pe, body)
                for i in TAIL:
                    for _, c in due(["forward"], i):
                        forward(NU - 1, c)

            @block.scalar
            def _(act):
                act.sem_inc(silu, BANKS)
                act.sem_inc(t_copied, 1)
                act.sem_inc(squared, 2 * SLOTS)
                G.start_scalar(act)

                def square(u, s, half):
                    n = 2 * (UNIT * u + s) + half
                    act.wait_ge(added, n + 1)
                    act.wait_ge(reduced, n + 1)
                    nc.scalar.activation(q[:, half], x1[:, s % SLOTS, HR * half:HR * (half + 1)], ACT.Square).then_inc(squared, 1)

                def t_copy(u, s):
                    act.wait_ge(summed, UNIT * u + s + 1 + SLOTS)
                    act.wait_ge(t_stored[s % 2], 32 * (UNIT // 2) * u + 32 * (s // 2) + 32)
                    for g in range(2):
                        rows = slice(C * g, C * g + L1.KYR)
                        last = nc.scalar.activation(ts[rows, s % 2], tp[rows], ACT.Copy)
                    last.then_inc(t_copied, 1)

                def x1_work(u, i, first):
                    for kind, c in due(["square0", "square1", "t_copy"], i, first):
                        t_copy(u, c) if kind == "t_copy" else square(u, c, int(kind[-1]))

                def body(b, half, after, new):
                    u, first, last = HALF * b + half, is_first(b), after is None
                    for i in range(STEPS):
                        s, m = i // BANKS, i % BANKS
                        n = UNIT * u + s
                        act.wait_ge(pixels, STEPS * u + i + 1)
                        if m == 0:
                            act.wait_ge(summed, n + 1)
                            act.wait_ge(squared, 2 * n + 2)
                            act.wait_ge(x1_stored[s % SLOTS], 32 * u + 16 * (s // SLOTS) + 16)
                        nc.scalar.activation(x1[:, s % SLOTS, BROWS * m:BROWS * (m + 1)].rearrange("p h c -> p (h c)"),
                                             z[:, m], ACT.Silu).then_inc(silu, 1)
                        if i in high_at and not last:
                            G.high(act, *high_at[i], after, 1 - half)
                        x1_work(u, i, first)

                units(act, body)
                for i in TAIL:
                    x1_work(NU - 1, i, False)

            @block.gpsimd
            def _(pool):
                with pool.Fori(0, NU) as u:
                    for s in range(UNIT):
                        for half in range(2):
                            rows = slice(HR * half, HR * (half + 1))
                            pool.wait_ge(silu, BANKS * (UNIT * u + s + 1) + 2 * (half + 1))
                            nc.gpsimd.tensor_tensor(x1[:, s % SLOTS, rows], x1[:, s % SLOTS, rows], x[:, s % SLOTS, rows],
                                                    ALU.add).then_inc(added, 1)

            @block.vector
            def _(dve):
                dve.sem_inc(reduced, 2)
                dve.sem_inc(final, 1)
                G.start_vector(dve)

                def reduce(u, s, half):
                    if s == 0 and half == 0:
                        dve.wait_ge(final, u + 1)
                    dve.wait_ge(squared, 2 * (UNIT * u + s) + half + 1 + 2 * SLOTS)
                    nc.vector.tensor_reduce(part[:, 2 * (s % UNIT) + half], q[:, half].rearrange("p h (j c) -> p c h j", j=J),
                                            AX.XY, ALU.add).then_inc(reduced, 1)

                def x1_work(u, i, first):
                    for kind, c in due(["reduce0", "reduce1", "total"], i, first):
                        if kind != "total":
                            reduce(u, c, int(kind[-1]))
                        elif c % UNIT == UNIT - 1:
                            v = u + c // UNIT
                            dve.wait_ge(reduced, 2 * UNIT * (v + 1) + 2)
                            nc.vector.tensor_reduce(sq[:, v], part[:].rearrange("p n c -> p c n"), AX.X, ALU.add).then_inc(final, 1)

                def body(b, half, after, new):
                    u, first, last = HALF * b + half, is_first(b), after is None
                    for i in range(STEPS):
                        s, m = i // BANKS, i % BANKS
                        dve.wait_ge(turned, STEPS * u + i + 1)
                        nc.vector.tensor_copy(xt[:, m % 2], pt[:, m % 2]).then_inc(turned_copied, 1)
                        if i in TURN_AT and new is not None:
                            G.turn(dve, new, TURN_AT[i])
                        if i in low_at and not last:
                            G.low(dve, *low_at[i], after, 1 - half)
                        x1_work(u, i, first)

                units(dve, body)
                for i in TAIL:
                    x1_work(NU - 1, i, False)


def pixels1(nc, lay, k, chunks, y_dram, out_dram):
    DEEP = chunks.slots
    with Tiles(nc, "p") as t:
        x, loaded = chunks.x, chunks.loaded
        z = t.ps("z", [P, 4, NB])
        G = InverseH(nc, lay, t, k, y_dram, [z[:, m] for m in range(4)], 4)
        stored = t.sems("stored", DEEP)
        spectral, added = t.sem("spectral"), t.sem("added")
        tabs = (k["inv_w1h"], k["inv_w1l"])
        NU = B * HALF
        STEPS = UNIT * BANKS
        APART = lay.NG + 1
        sums_at = {1 + APART * r: r for r in range(lay.RR)}
        high_at = {1 + APART * r + g: (r, g) for r in range(lay.RR) for g in range(lay.NG)}
        low_at = {2 + APART * r + g: (r, g) for r in range(lay.RR) for g in range(lay.NG)}
        assert max(low_at) < STEPS
        TURN_AT = {STEPS - G.TURNS + n: n for n in range(G.TURNS)}

        with nc.Block() as block:
            @block.sync
            def _(sp):
                def body(b, half, after, new):
                    u, last = HALF * b + half, after is None
                    for s in range(DEEP):
                        if is_first(b):
                            continue
                        if s == 1 and new is not None:
                            G.load(sp, new)
                        sp.wait_ge(stored[s], 16 * (u + 1))
                        chunks.load(sp, UNIT * u + s, s)

                G.load(sp, 0)
                for s in range(len(chunks.early), DEEP):
                    chunks.load(sp, s, s)
                G.load(sp, 1)
                units(sp, body)

            @block.tensor
            def _(pe):
                G.start_tensor(pe)

                def body(b, half, after, new):
                    u, last = HALF * b + half, after is None
                    G.complete(pe, b, half)
                    for i in range(STEPS):
                        pe.wait_ge(added, STEPS * u + i + 1)
                        G.inverse_w(tabs, z[:, i % BANKS], half, BROWS * i).then_inc(spectral, 1)
                        if i in sums_at and not last:
                            G.tensor(pe, sums_at[i], after, 1 - half)

                units(pe, body)

            @block.vector
            def _(dve):
                dve.sem_inc(added, BANKS)
                G.start_vector(dve)

                def body(b, half, after, new):
                    u, last = HALF * b + half, after is None
                    for i in range(STEPS):
                        s, m = i // BANKS, i % BANKS
                        if m == 0:
                            dve.wait_ge(loaded[s], LOADED * u + LOADED)
                        dve.wait_ge(spectral, STEPS * u + i + 1)
                        rows = x[:, s, BROWS * m:BROWS * (m + 1)].rearrange("p h c -> p (h c)")
                        nc.vector.tensor_tensor(rows, rows, z[:, m], ALU.add).then_inc(added, 1)
                        if i in TURN_AT and new is not None:
                            G.turn(dve, new, TURN_AT[i])
                        if i in low_at and not last:
                            G.low(dve, *low_at[i], after, 1 - half)

                units(dve, body)

            @block.scalar
            def _(act):
                for s in range(DEEP):
                    act.sem_inc(stored[s], 16)
                G.start_scalar(act)

                def body(b, half, after, new):
                    u, last = HALF * b + half, after is None
                    for i in range(STEPS):
                        s, m = i // BANKS, i % BANKS
                        if i in high_at and not last:
                            G.high(act, *high_at[i], after, 1 - half)
                        if m == BANKS - 1:
                            act.wait_ge(added, STEPS * u + i + 1 + BANKS)
                            act.dma_start(out_dram[UNIT * u + s], x[:, s]).then_inc(stored[s], 16)

                units(act, body)
                for s in range(DEEP):
                    act.wait_ge(stored[s], 16 * (NU + 1))


def build(nc, d, out):
    def scratch(name, shape):
        return nc.dram_tensor(name, shape, F32, kind="Internal").ap()

    t0 = scratch("t0", [L0.KYR, B * H, C])
    t1 = scratch("t1", [L1.KYR, B * H, C])
    x0h, y0 = scratch("x0h", [2, RI, B, L0.M // 2, C]), scratch("y0", [RI, B, L0.M, C])
    x1h, y1 = scratch("x1h", [2, RI, B, L1.M // 2, C]), scratch("y1", [RI, B, L1.M, C])
    x1 = scratch("x1", [NCH, P, ROWS * JC])
    image = lambda a: a.rearrange("b (k h) (p j) c -> (b k) p h (j c)", k=CHUNKS, j=J)
    by_image = lambda a: a.rearrange("r b (x y) c -> r b x (y c)", x=KX)
    by_half = lambda a: a.rearrange("a r b (x y) c -> a r b x (y c)", x=KX // 2)
    by_octet = lambda a: a.rearrange("a r b (m q) c -> a (r b m) (q c)", m=8)
    by_round = lambda a: a.rearrange("r b (a n g m) c -> g n (r b) a (m c)", a=2, g=4, m=4)
    t_rows = lambda a: a.rearrange("k (n h) c -> n k (h c)", h=8)
    t_pairs = lambda a: a.rearrange("k (b p e) c -> b p k (e c)", p=P, e=PAIR)

    with Tiles(nc, "k") as t:
        k = {"ident": t.sb("ident", [P, P]), "fwd_h": t.sb("fwd_h", [P, HALF * 2 * 2 * KX]),
             "inv_h": t.sb("inv_h", [RI * KX, H]), "pairs": t.sb("pairs", [C, P]), "ones": t.sb("ones", [P, 8]),
             "wdiag": t.sb("wdiag", [P, P]), "wres": t.sb("wres", [C, C]), "bias": t.sb("bias", [B, C]),
             "wscaled": t.sb("wscaled", [P, B, P])}
        for n, lay in enumerate((L0, L1)):
            k[f"fwd_w{n}"] = t.sb(f"fwd_w{n}", [P, J * lay.KYR])
            if n:
                k[f"inv_w{n}h"] = t.sb(f"inv_w{n}h", [lay.K, J * P], F32R)
                k[f"inv_w{n}l"] = t.sb(f"inv_w{n}l", [lay.K, J * P], F32R)
        k["inv_w0"] = t.sb("inv_w0", [P, J * P], F32R)
        sq = t.sb("sq", [P, B * HALF, C])
        with Tiles(nc, "w0") as tw:
            wt = Weights0(nc, L0, tw, [d[n].rearrange("i o (a x) y r -> a i o (x y r)", a=Weights0.PARTS) for n in ("fw0", "fw1")])
            with Tiles(nc, "x") as tx:
                chunks = Chunks(tx, SLOTS, image(d["x"]), SLOTS)
                load_constants(nc, d, k, chunks)
                forward_w0(nc, L0, k, chunks, t_rows(t0), sq, wt)
            forward_h(nc, L0, "h0", k, t_pairs(t0), by_half(x0h))
            mix_modes(nc, L0, "m0", k, sq, by_octet(x0h), by_round(y0), wt)
        pixels0(nc, L0, k, image(d["x"]), by_image(y0), x1, t_rows(t1), sq)
        with Tiles(nc, "x1") as tx:
            chunks = Chunks(tx, UNIT, x1.rearrange("n p (h c) -> n p h c", h=ROWS), 3)
            with Tiles(nc, "w1") as tw:
                wt = Weights1(nc, L1, tw, k, [d[n].rearrange("x y o i -> (x y) o i").rearrange("(a n q) o i -> a n o q i", a=2, q=4 * L1.RM)
                                              for n in ("kernel_re", "kernel_im")])
                forward_h(nc, L1, "h1", k, t_pairs(t1), by_half(x1h))
                mix_modes(nc, L1, "m1", k, sq, by_octet(x1h), by_round(y1), wt, chunks)
            pixels1(nc, L1, k, chunks, by_image(y1), image(out))


def kernel(x, L0_conv_W_res, L0_conv_b_res, L0_conv_fw0, L0_conv_fw1, L1_conv_kernel_re, L1_conv_kernel_im):
    import concourse.bacc as bacc
    from concourse.bass_utils import run_bass_kernel_spmd

    nc = bacc.Bacc("TRN2", target_bir_lowering=False, num_devices=1)
    arrays = {"x": x, "W_res": L0_conv_W_res, "b_res": L0_conv_b_res, "fw0": L0_conv_fw0, "fw1": L0_conv_fw1,
              "kernel_re": L1_conv_kernel_re, "kernel_im": L1_conv_kernel_im}
    arrays = {n: np.ascontiguousarray(a) for n, a in arrays.items()} | tables()
    maps, d = {}, {}
    for n, a in arrays.items():
        maps[f"in_{n}"] = a
        d[n] = nc.dram_tensor(f"in_{n}", a.shape, mybir.dt.from_np(a.dtype), kind="ExternalInput").ap()
    out = nc.dram_tensor("out", (B, H, W, C), F32, kind="ExternalOutput").ap()
    build(nc, d, out)
    r = run_bass_kernel_spmd(nc, [maps], core_ids=[0])
    return r.results[0]["out"]
```
